# Optimizing a Trainium2 kernel written in Bass

```python
import numpy as np
import jax
import jax.numpy as jnp

def _softmax(x, axis=-1):
    return jax.nn.softmax(x, axis=axis)

def _gelu(x):
    return jax.nn.gelu(x, approximate=True)

def _silu(x):
    return jax.nn.silu(x)

def _sigmoid(x):
    return jax.nn.sigmoid(x)

def _layernorm(x, axis=-1, eps=1e-05):
    m = jnp.mean(x, axis=axis, keepdims=True)
    v = jnp.var(x, axis=axis, keepdims=True)
    return (x - m) / jnp.sqrt(v + eps)

def _scatter_add(tgt, idx, src, axis=0):
    return tgt.at[idx].add(src)

def _segment_sum(src, seg, n):
    return jax.ops.segment_sum(src, seg, n)
kernel_name = 'mk_prb_d1_jaxref_r8_dca872'

def setup_inputs(seed: int=0):
    np.random.seed(seed)
    _w = jnp.asarray

    def _L0_attn_setup():
        import jax, jax.numpy as jnp
        import numpy as np
        EMB = 128
        HEADS = 16
        HEAD_SIZE = EMB // HEADS
        B, T = (2, 256)
        key = jax.random.key(seed)
        k1, k2, k3 = jax.random.split(key, 3)
        x = jax.random.normal(k1, (B, T, EMB), dtype=jnp.float32)
        w_qkv = jax.random.normal(k2, (EMB, 3 * EMB), dtype=jnp.float32) * EMB ** (-0.5)
        w_proj = jax.random.normal(k3, (EMB, EMB), dtype=jnp.float32) * EMB ** (-0.5)
        b_proj = jnp.zeros((EMB,), dtype=jnp.float32)
        return {'x': x, 'w_qkv': w_qkv, 'w_proj': w_proj, 'b_proj': b_proj}
    _L0_attn_in = _L0_attn_setup()

    def _L0_ffn_setup():
        import jax, jax.numpy as jnp
        import numpy as np
        HIDDEN = 128
        INTER = 512
        N_EXPERTS = 8
        TOP_K = 2
        INIT_STD = 0.02
        key = jax.random.key(seed)
        ks = jax.random.split(key, 6)
        x = jax.random.normal(ks[0], (2, 128, HIDDEN), dtype=jnp.float32)
        Wg = jax.random.normal(ks[1], (N_EXPERTS, HIDDEN), dtype=jnp.float32) * INIT_STD
        W1 = jax.random.normal(ks[2], (N_EXPERTS, HIDDEN, INTER), dtype=jnp.float32) * INIT_STD
        b1 = jnp.zeros((N_EXPERTS, INTER), dtype=jnp.float32)
        W2 = jax.random.normal(ks[3], (N_EXPERTS, INTER, HIDDEN), dtype=jnp.float32) * INIT_STD
        b2 = jnp.zeros((N_EXPERTS, HIDDEN), dtype=jnp.float32)
        return {'x': x, 'Wg': Wg, 'W1': W1, 'b1': b1, 'W2': W2, 'b2': b2}
    _L0_ffn_in = _L0_ffn_setup()
    _d = {'L0_attn_x': _L0_attn_in['x'], 'L0_attn_w_qkv': _L0_attn_in['w_qkv'], 'L0_attn_w_proj': _L0_attn_in['w_proj'], 'L0_attn_b_proj': _L0_attn_in['b_proj'], 'L0_ffn_Wg': _L0_ffn_in['Wg'], 'L0_ffn_W1': _L0_ffn_in['W1'], 'L0_ffn_b1': _L0_ffn_in['b1'], 'L0_ffn_W2': _L0_ffn_in['W2'], 'L0_ffn_b2': _L0_ffn_in['b2']}
    _x0 = _d['L0_attn_x']
    _d['L0_attn_x'] = jax.random.normal(jax.random.fold_in(jax.random.key(seed), 1), (4, 1024, 128), dtype=_x0.dtype)
    del _x0
    return _d

def reference(L0_attn_x, L0_attn_w_qkv, L0_attn_w_proj, L0_attn_b_proj, L0_ffn_Wg, L0_ffn_W1, L0_ffn_b1, L0_ffn_W2, L0_ffn_b2):

    def _L0_attn_ref(x, w_qkv, w_proj, b_proj):
        import jax, jax.numpy as jnp
        import numpy as np
        EMB = 128
        HEADS = 16
        HEAD_SIZE = EMB // HEADS
        B, T = (2, 256)
        Bb, Tt, C = x.shape
        qkv = x @ w_qkv
        q, k, v = jnp.split(qkv, 3, axis=-1)
        q = q.reshape(Bb, Tt, HEADS, HEAD_SIZE).transpose(0, 2, 1, 3)
        k = k.reshape(Bb, Tt, HEADS, HEAD_SIZE).transpose(0, 2, 1, 3)
        v = v.reshape(Bb, Tt, HEADS, HEAD_SIZE).transpose(0, 2, 1, 3)
        scale = HEAD_SIZE ** (-0.5)
        wei = jnp.einsum('bhqd,bhkd->bhqk', q, k) * scale
        causal = jnp.tril(jnp.ones((Tt, Tt), dtype=bool))
        wei = jnp.where(causal, wei, -jnp.inf)
        wei = jax.nn.softmax(wei, axis=-1)
        out = jnp.einsum('bhqk,bhkd->bhqd', wei, v)
        out = out.transpose(0, 2, 1, 3).reshape(Bb, Tt, C)
        out = out @ w_proj + b_proj
        return out

    def _L0_ffn_ref(x, Wg, W1, b1, W2, b2):
        import jax, jax.numpy as jnp
        import numpy as np
        HIDDEN = 128
        INTER = 512
        N_EXPERTS = 8
        TOP_K = 2
        INIT_STD = 0.02
        orig_shape = x.shape
        xt = x.reshape(-1, HIDDEN)
        T = xt.shape[0]
        logits = xt @ Wg.T
        topk_logits, topk_idx = jax.lax.top_k(logits, TOP_K)
        w = jax.nn.softmax(topk_logits, axis=-1)
        rows = jnp.arange(T)[:, None]
        gates = jnp.zeros((T, N_EXPERTS), xt.dtype).at[rows, topk_idx].add(w)
        h = jnp.einsum('th,ehi->tei', xt, W1) + b1
        h = jax.nn.gelu(h, approximate=False)
        o = jnp.einsum('tei,eih->teh', h, W2) + b2
        y = jnp.einsum('te,teh->th', gates, o)
        return y.reshape(orig_shape)
    x = L0_attn_x
    xn = _layernorm(x, axis=-1)
    x = x + _L0_attn_ref(xn, L0_attn_w_qkv, L0_attn_w_proj, L0_attn_b_proj) + _L0_ffn_ref(xn, L0_ffn_Wg, L0_ffn_W1, L0_ffn_b1, L0_ffn_W2, L0_ffn_b2)
    return x

_drawn_inputs = setup_inputs


def setup_inputs(seed=0):
    import zlib

    import numpy as np

    out = dict(_drawn_inputs(seed))
    spreads = {'L0_attn_b_proj': (0.0, 0.1), 'L0_ffn_b1': (0.0, 0.483), 'L0_ffn_b2': (0.0, 0.1)}
    factors = {}
    for name, (base, spread) in spreads.items():
        noise = np.random.default_rng([zlib.crc32(name.encode()), seed]).standard_normal(out[name].shape)
        drawn = base * np.exp(spread * noise) if base else spread * noise
        out[name] = jnp.asarray(drawn.astype(out[name].dtype))
    for name, factor in factors.items():
        out[name] = (out[name] * factor).astype(out[name].dtype)
    return out
```

```python
from contextlib import ExitStack

import concourse.bass as bass
import numpy as np
from concourse import mybir

F32 = mybir.dt.float32
F32R = mybir.dt.float32r
ACT = mybir.ActivationFunctionType
ALU = mybir.AluOpType
AX = mybir.AxisListType

B, T, C = 4, 1024, 128
TOK = B * T
P = 128
NT = TOK // P
TPB = T // P
H, D = 16, 8
HG = 4
G4 = H // HG
E, I = 8, 512
CH = I // P
EG = 4
NH = EG * CH
W = 512
EPS = 1e-5
SCALE = float(D) ** -0.5
CONSTS = 2 * P + 6 + E
LOW = -3.0e38
MASKED = -1.0e30

SUB = [(0, j, P * j, W - P * j) for j in range(4)] + [(1, j, W, W) for j in range(4)] + \
      [(1, j, P * j, T - P * j) for j in range(4, TPB)]
NS = len(SUB)
DIAG = [s for s, (c, j, q, n) in enumerate(SUB) if q == P * j]
MAXES = [(i, 0, P * (i + 1), True, 0) for i in range(4)] + \
        [x for i in range(4, TPB) for x in ((i, 0, W, False, 1), (i, W, P * (i + 1) - W, True, 0))]
YCHUNKS = [[0, 1, 2], [3], [4], [5, 6], [7], [8], [9], [10], [11], [12], [13], [14, 15]]
YEND = {s: x[-1] // CH for s, x in enumerate(YCHUNKS) if x[-1] % CH == CH - 1}
AFTER = {2: ("madd1", 0), 3: ("ot1", 0), 4: ("prep", 0), 5: ("ft", 0), 6: ("prep", 1), 7: ("ft", 1),
         8: ("prep", 2), 10: ("prep", 3), 11: ("fo", 0), 13: ("fo", 1)}
SC_UNITS = NH + HG * NS
MAX_UNITS = HG * NS
AUX_START = 4 + MAX_UNITS + 1


def present(what, g, first, last):
    if what == "prep":
        return not (last and g == G4 - 1)
    if what == "ot1":
        return not (first and g == 0)
    if what in ("ft", "fo"):
        return g == 0 and not first
    return True


def aux_order(first, last):
    names = []
    for g in range(G4):
        for k in sorted(AFTER):
            what, u = AFTER[k]
            if present(what, g, first, last):
                names.append((what, g, u))
        for s in range(NS):
            more = present("prep", g, first, last)
            names += [("max", g, s, h) for h in range(HG - 1) if more]
            if s == 5 and more:
                names.append(("madd0", g))
            if s == 7:
                names.append(("ot0", g))
            if more:
                names.append(("max", g, s, HG - 1))
    return {name: i for i, name in enumerate(names)}


def aux_base(b):
    if isinstance(b, int) and b == 0:
        return AUX_START
    whole = len(aux_order(False, False))
    return b * whole + (AUX_START + len(aux_order(True, False)) - whole)


def aux_parity(b):
    return aux_base(b if isinstance(b, int) else 1) % 2


def wait(eng, sem, value):
    if not isinstance(value, int) or value > 0:
        eng.wait_ge(sem, value)


def bcast(ap, n):
    return ap.unsqueeze(len(ap.shape)).to_broadcast([*ap.shape, n])


def layer_kernel(nc, x, w_qkv, w_proj, b_proj, Wg, W1, b1, W2, b2, consts, out):
    ctx = ExitStack()
    with ctx:
        def sb(name, shape, dt=F32):
            return ctx.enter_context(nc.sbuf_tensor(name, shape, dt))

        def sem(name):
            return ctx.enter_context(nc.semaphore(name))

        cst = sb("cst", [P, CONSTS])
        ident, cmask = cst[:, 0:P], cst[:, P:2 * P]
        lo_row = [cst[:, 2 * P + 2 * kq:2 * P + 2 * kq + 1] for kq in range(2)]
        hi_sign = [cst[:, 2 * P + 2 * kq + 1:2 * P + 2 * kq + 2] for kq in range(2)]
        ones_row = [cst[:, 2 * P + 4 + kq:2 * P + 5 + kq] for kq in range(2)]
        w1h, w1l = sb("w1h", [P, E, I], F32R), sb("w1l", [P, E, I], F32R)
        w2 = sb("w2", [P, E * CH, C])
        wkqh, wkql = sb("wkqh", [P, 2, G4, P], F32R), sb("wkql", [P, 2, G4, P], F32R)
        wvgh, wvgl = sb("wvgh", [P, C + E], F32R), sb("wvgl", [P, C + E], F32R)
        wvg = sb("wvg", [P, C + E])
        wqkv = sb("wqkv", [P, 3 * C])
        wp, bp = sb("wp", [P, C]), sb("bp", [P, C])
        small = sb("small", [P, P])
        smallT = sb("smallT", [P, 72])
        b1T, b2T, wgT = smallT[:, 0:32], smallT[:, 32:40], smallT[:, 64:72]
        xh, xl = sb("xh", [P, TOK], F32R), sb("xl", [P, TOK], F32R)
        kT = [sb(f"kT{i}", [P, T], F32R) for i in range(2)]
        qT = [sb(f"qT{i}", [P, T], F32R) for i in range(2)]
        v = [sb(f"v{i}", [P, TPB, HG, 32]) for i in range(2)]
        hic = sb("hic", [P, 2, W])
        vst = sb("vst", [P, TPB, 32])
        probs = sb("probs", [P, 2, HG, W])
        maxes = sb("maxes", [P, TPB, 3, HG])
        mrow = sb("mrow", [P, 4, HG])
        mspread = sb("mspread", [P, 4, P])
        junk = sb("junk", [P, 2, P])
        ot = sb("ot", [P, 2, W])
        rden = sb("rden", [P, 4, HG])
        attn = sb("attn", [P, TPB, G4, HG, D])
        attnT = sb("attnT", [P, T])
        hid = sb("hid", [P, NH, W])
        gates = sb("gates", [P, 4, EG, P])
        ytmp = sb("ytmp", [P, 2, W])
        yT = sb("yT", [P, T])
        xres = sb("xres", [P, 2, 4, C])
        x_in = hid[:, 0:8, :].rearrange("p a (b c) -> p (a b) c", c=C)
        w1_in = hid[:, 8:16, :]
        wkq = ytmp[:, :, :].rearrange("p a (g r) -> p a g r", r=P)
        v_all = probs[:, :, :, :].rearrange("p a b w -> p (a b w)") \
            .rearrange("p (n g t c) -> p n g t c", n=B, g=G4, c=32)
        stats = attnT[:, 0:NT * 6].rearrange("p (t s) -> p t s", s=6)
        meanvar = attnT[:, NT * 6:NT * 8].rearrange("p (t s) -> p t s", s=2)
        rstd = attnT[:, NT * 8:NT * 9]
        veps = attnT[:, NT * 9:NT * 10]
        half = attnT[:, NT * 10:NT * 11]
        gt = gates[:, :, :, :].rearrange("p t e q -> p (t e q)")

        def gtile(i):
            return gt[:, i * NT * E:(i + 1) * NT * E].rearrange("p (t e) -> p t e", e=E)

        logits, eq, first1, rest, first2 = (gtile(i) for i in range(5))
        grow = ot[:, 0, 0:2 * P].rearrange("p (k q) -> p k q", k=2)
        g_all = ytmp[:, 1, 0:NT * E].rearrange("p (t e) -> p t e", e=E)
        gcol = attn[:, :, :, :, :].rearrange("p a b c d -> p (a b c d)")
        rank8 = cst[:, 2 * P + 6:2 * P + 6 + E]
        top1, top2, c1, c2, dlt, ex, den, r1, r2 = (gcol[:, 32 + 32 * i:64 + 32 * i] for i in range(9))

        sc = [ctx.enter_context(nc.psum_tensor(f"sc{i}", [P, W], F32)) for i in range(4)]
        aux = [ctx.enter_context(nc.psum_tensor(f"aux{i}", [P, W], F32)) for i in range(2)]
        ov = ctx.enter_context(nc.psum_tensor("ov", [P, W], F32))
        yp = ctx.enter_context(nc.psum_tensor("yp", [P, W], F32))

        v_scr = nc.dram_tensor("v_scr", [B * G4, P, TPB * 32], F32, kind="Internal").ap()
        g_scr = nc.dram_tensor("g_scr", [NT, E * P], F32, kind="Internal").ap()
        x_v = x.rearrange("b (n i p) c -> (b n) p i c", i=4, p=P)
        out_v = out.rearrange("b (n i p) c -> (b n) p i c", i=4, p=P)

        x_loaded = [sem(f"x_loaded{i}") for i in range(4)]
        c_loaded, s_loaded, w_loaded = sem("c_loaded"), sem("s_loaded"), sem("w_loaded")
        w1_loaded, w2_loaded, p_loaded = sem("w1_loaded"), sem("w2_loaded"), sem("p_loaded")
        chain = sem("chain")
        pchain = sem("pchain")
        small_zero, smallT_ready, smallT_done = sem("small_zero"), sem("smallT_ready"), sem("smallT_done")
        mv_ready, rstd_ready, xn_ready = sem("mv_ready"), sem("rstd_ready"), sem("xn_ready")
        xT_ready, xh_done, xl_done = sem("xT_ready"), sem("xh_done"), sem("xl_done")
        wkq_ready, wvg_ready, w1h_done, w1l_done = sem("wkq_ready"), sem("wvg_ready"), sem("w1h_done"), sem("w1l_done")
        vg_ready, vg_done, v_stored = sem("vg_ready"), sem("vg_done"), sem("v_stored")
        dlt_ready, ex_ready, g_ready, gT_ready, gT_done, g_stored = (
            sem(n) for n in ("dlt_ready", "ex_ready", "g_ready", "gT_ready", "gT_done", "g_stored"))
        zeroed = sem("zeroed")
        sc_ready, act_done = sem("sc_ready"), sem("act_done")
        aux_ready, aux_done = sem("aux_ready"), sem("aux_done")
        hic_done = sem("hic_done")
        mrow_done, negh_done, msp_ready = sem("mrow_done"), sem("negh_done"), sem("msp_ready")
        sel_done, pv_done, ot_evac, rden_done = sem("sel_done"), sem("pv_done"), sem("ot_evac"), sem("rden_done")
        vst_loaded, v_done = sem("vst_loaded"), sem("v_done")
        y_done, ymul_done, yadd_done, gates_loaded = sem("y_done"), sem("ymul_done"), sem("yadd_done"), sem("gates_loaded")
        xres_loaded, xb_done, stored = sem("xres_loaded"), sem("xb_done"), sem("stored")

        dve_turn, pool_turn = sem("dve_turn"), sem("pool_turn")
        block = ctx.enter_context(nc.Block())

        def over_batches(eng, body):
            body(0, True, False)
            with eng.Fori(1, B - 1) as b:
                body(b, False, False)
            body(B - 1, False, True)

        def load_v(sp, n):
            sp.dma_start(vst[:, :, :].rearrange("p t c -> p (t c)"),
                         v_scr[bass.ds(n, 1)].rearrange("o p f -> p (o f)")).then_inc(vst_loaded, 16)

        def load_gates(sp, b, g):
            e0 = EG * (g % 2)
            sp.dma_start(gates[:, :, :, :].rearrange("p t e q -> p t (e q)"),
                         g_scr[bass.ds(b * TPB + g // 2 * 4, 4), e0 * P:(e0 + EG) * P].partition_broadcast(P)) \
                .then_inc(gates_loaded, 16)

        def load_xres(sp, b):
            for c in range(2):
                sp.dma_start(xres[:, c], x_v[bass.ds(2 * b - 2 + c, 1)].rearrange("o p i c -> p (o i) c")) \
                    .then_inc(xres_loaded, 16)

        def store(sp, b, c):
            sp.dma_start(out_v[bass.ds(2 * b - 2 + c, 1)].rearrange("o p i c -> p (o i) c"), xres[:, c]) \
                .then_inc(stored, 16)

        def sync_batch(b, first, last):
            sp, order, base = nc.sync, aux_order(first, last), aux_base(b)
            for g in range(G4):
                n = G4 * b + g
                if g == 0 and not first:
                    wait(sp, stored, 32 * b - 32)
                    load_xres(sp, b)
                if present("prep", g, first, last):
                    sp.wait_ge(v_done, n + 1)
                    load_v(sp, n + 1)
                if g == 0 and not first:
                    for c in range(2):
                        sp.wait_ge(aux_done, base + order["fo", 0, c] + 1)
                        store(sp, b, c)
                if present("prep", g, first, last):
                    sp.wait_ge(ymul_done, EG * n + EG)
                    load_gates(sp, b + (g + 1) // G4, (g + 1) % G4)

        def expand_v(pool, n, parity):
            pool.wait_ge(zeroed, 5)
            pool.wait_ge(vst_loaded, 16 * (n + 1))
            wait(pool, pv_done, NS * (n - 1))
            if not isinstance(n, int):
                pool.sem_inc(pool_turn, 1)
            nc.gpsimd.tensor_copy(v[parity][:, :, :, 0:D],
                                  vst[:, :, :].rearrange("p t (h d) -> p t h d", d=D)).then_inc(v_done, 1)

        def finish_bias(pool, b):
            pool.wait_ge(xres_loaded, 32 * b)
            wait(pool, p_loaded, 32)
            for c in range(2):
                nc.gpsimd.tensor_tensor(xres[:, c], xres[:, c],
                                        bp[:, :].unsqueeze(1).to_broadcast([P, 4, C]), ALU.add).then_inc(xb_done, 1)

        def pool_batch(b, first, last):
            pool = nc.gpsimd
            for g in range(G4):
                n = G4 * b + g
                if present("prep", g, first, last):
                    expand_v(pool, n + 1, (g + 1) % 2)
                if g == 0 and not first:
                    finish_bias(pool, b)
                for s in range(NS):
                    if s in DIAG:
                        pool.wait_ge(act_done, SC_UNITS * n + NH + HG * (s + 1))
                        if not isinstance(n, int):
                            pool.sem_inc(pool_turn, 1)
                        block_ = probs[:, s % 2, :, 0:P]
                        nc.gpsimd.affine_select(out=block_, in_=block_, compare_op=ALU.is_ge, fill=0.0, base=0,
                                                pattern=[[0, HG], [1, P]], channel_multiplier=-1).then_inc(sel_done, 1)
                    if s in YEND:
                        e = EG * (g % 2) + YEND[s]
                        if e > 0:
                            half_ = yT[:, W * (g // 2):W * (g // 2 + 1)]
                            adds = (E - 1) * (2 * b + g // 2) + e - 1
                            pool.wait_ge(ymul_done, EG * n + YEND[s] + 1)
                            wait(pool, yadd_done, adds)
                            nc.gpsimd.tensor_tensor(half_, half_, ytmp[:, e % 2, :], ALU.add).then_inc(yadd_done, 1)

        def prep_hic(act, u, unit, bank, before):
            act.wait_ge(aux_ready, unit + 1)
            if u >= 2:
                act.wait_ge(aux_done, before + 1)
            nc.scalar.activation(hic[:, u % 2, :].bitcast(F32R), aux[bank][:, :], ACT.Identity,
                                 bias=ones_row[u % 2], scale=hi_sign[u % 2]).then_inc(hic_done, 1)

        def evacuate_ov(act, n, c):
            act.wait_ge(pv_done, NS * n + (4 if c == 0 else NS))
            wait(act, rden_done, 2 * n + c - 1)
            nc.scalar.copy(ot[:, c, :], ov[:, :]).then_inc(ot_evac, 1)

        def act_batch(b, first, last):
            act, order, base = nc.scalar, aux_order(first, last), aux_base(b)
            for g in range(G4):
                n = G4 * b + g
                start = SC_UNITS * n
                wait(act, y_done, EG * n)
                for k in range(NH):
                    act.wait_ge(sc_ready, start + k + 1)
                    nc.scalar.activation(hid[:, k, :], sc[k % 4][:, :], ACT.Gelu,
                                         bias=b1T[:, NH * (g % 2) + k:NH * (g % 2) + k + 1]).then_inc(act_done, 1)
                    if k == 1 and not (first and g == 0):
                        evacuate_ov(act, n - 1, 1)
                    what, u = AFTER.get(k, (None, 0))
                    if what == "prep" and present(what, g, first, last):
                        o = order[what, g, u]
                        prep_hic(act, u, base + o, (aux_parity(b) + o) % 2,
                                 base + order[what, g, max(u - 2, 0)])
                for s, (_, _, _, cols) in enumerate(SUB):
                    wait(act, pv_done, NS * n + s - 1)
                    for h in range(HG):
                        k = NH + HG * s + h
                        act.wait_ge(sc_ready, start + k + 1)
                        nc.scalar.activation(probs[:, s % 2, h, 0:cols], sc[k % 4][:, 0:cols],
                                             ACT.Exp).then_inc(act_done, 1)
                    if s == 4:
                        if first and g == 0:
                            act.wait_ge(g_stored, 32)
                        evacuate_ov(act, n, 0)

        def split_product(out_, wh, wl, mh, ml):
            nc.tensor.matmul(out_, wh, mh, start=True, stop=False)
            nc.tensor.matmul(out_, wh, ml, start=False, stop=False)
            return nc.tensor.matmul(out_, wl, mh, start=False, stop=True)

        def aux_free(pe, unit):
            wait(pe, aux_done, unit - 1)

        def prep_product(pe, g, u, unit, bank, token):
            aux_free(pe, unit)
            tok = bass.ds(token + W * (u // 2), W)
            split_product(aux[bank][:, :], wkqh[:, u % 2, g, :], wkql[:, u % 2, g, :],
                          xh[:, tok], xl[:, tok]).then_inc(aux_ready, 1)

        def max_scores(pe, s, h, parity, unit, bank):
            i, k0, cols, _, _ = MAXES[s]
            rows = slice(32 * h, 32 * h + 32)
            aux_free(pe, unit)
            nc.tensor.matmul(aux[bank][:, 0:cols], qT[parity][rows, P * i:P * i + P],
                             kT[parity][rows, k0:k0 + cols], start=True, stop=True).then_inc(aux_ready, 1)

        def scores(pe, g, s, start, heads):
            _, j, q, cols = SUB[s]
            for h in heads:
                k = NH + HG * s + h
                rows = slice(32 * h, 32 * h + 32)
                wait(pe, act_done, start + k - 3)
                nc.tensor.matmul(sc[k % 4][:, 0:cols], kT[g % 2][rows, P * j:P * j + P],
                                 qT[g % 2][rows, q:q + cols], start=True, stop=True).then_inc(sc_ready, 1)

        def max_rows(pe, m, c, unit, bank):
            aux_free(pe, unit)
            pe.wait_ge(msp_ready, 2 * m + c + 1)
            for t in range(4):
                last_ = nc.tensor.transpose(aux[bank][:, P * t:P * t + P], mspread[:, t, :], ident)
            last_.then_inc(aux_ready, 1)

        def values(pe, n, s, parity):
            c, j, q, cols = SUB[s]
            if j == 0:
                wait(pe, ot_evac, 2 * n + c)
            if s == 0:
                pe.wait_ge(v_done, n + 1)
            if s in DIAG:
                pe.wait_ge(sel_done, len(DIAG) * n + DIAG.index(s) + 1)
            else:
                pe.wait_ge(act_done, SC_UNITS * n + NH + HG * (s + 1))
            for h in range(HG):
                last_ = nc.tensor.matmul(ov[32 * h:32 * h + 32, W - cols:W], v[parity][:, j, h, :],
                                         probs[:, s % 2, h, 0:cols], start=(j == 0),
                                         stop=(j == (3 if c == 0 else TPB - 1)))
            last_.then_inc(pv_done, 1)

        def out_rows(pe, n, c, unit, bank):
            aux_free(pe, unit)
            pe.wait_ge(ot_evac, 2 * n + c + 1)
            for t in range(4):
                last_ = nc.tensor.transpose(aux[bank][:, P * t:P * t + P], ot[:, c, P * t:P * t + P], ident)
            last_.then_inc(aux_ready, 1)

        def attn_columns(pe, c, unit, bank, attn_unit):
            aux_free(pe, unit)
            pe.wait_ge(aux_done, attn_unit + 1)
            for t in range(4):
                last_ = nc.tensor.transpose(aux[bank][:, P * t:P * t + P],
                                            attn[:, 4 * c + t].rearrange("p g h d -> p (g h d)"), ident)
            last_.then_inc(aux_ready, 1)

        def project(pe, b, c, unit, bank, column_unit):
            aux_free(pe, unit)
            pe.wait_ge(aux_done, column_unit + 1)
            wait(pe, yadd_done, 2 * (E - 1) * b)
            for t in range(4):
                tok = slice(W * c + P * t, W * c + P * t + P)
                dst = aux[bank][:, P * t:P * t + P]
                nc.tensor.matmul(dst, attnT[:, tok], wp[:, :], start=True, stop=False)
                last_ = nc.tensor.matmul(dst, yT[:, tok], ident, start=False, stop=True)
            last_.then_inc(aux_ready, 1)

        def tensor_batch(b, first, last):
            pe, order, base, par = nc.tensor, aux_order(first, last), aux_base(b), aux_parity(b)
            for g in range(G4):
                n = G4 * b + g
                start = SC_UNITS * n
                token = b * T + W * (g // 2)
                for k in range(NH):
                    e, ch = EG * (g % 2) + k // CH, k % CH
                    wait(pe, act_done, start + k - 3)
                    split_product(sc[k % 4][:, :], w1h[:, e, P * ch:P * ch + P], w1l[:, e, P * ch:P * ch + P],
                                  xh[:, bass.ds(token, W)], xl[:, bass.ds(token, W)]).then_inc(sc_ready, 1)
                    if k == 0 and not (first and g == 0):
                        values(pe, n - 1, NS - 1, (g + 1) % 2)
                    what, u = AFTER.get(k, (None, 0))
                    if what is None or not present(what, g, first, last):
                        continue
                    o = order[what, g, u]
                    unit, bank = base + o, (par + o) % 2
                    if what == "madd1":
                        max_rows(pe, n, 1, unit, bank)
                    elif what == "ot1":
                        out_rows(pe, n - 1, 1, unit, bank)
                    elif what == "prep":
                        prep_product(pe, (g + 1) % G4, u, unit, bank, T * (b + (g + 1) // G4))
                    elif what == "ft":
                        attn_columns(pe, u, unit, bank, base + order["ot1", g, 0])
                    elif what == "fo":
                        project(pe, b, u, unit, bank, base + order["ft", g, u])
                more = present("prep", g, first, last)

                def max_unit(pe, s, h):
                    o = order["max", g, s, h]
                    max_scores(pe, s, h, (g + 1) % 2, base + o, (par + o) % 2)

                pe.wait_ge(aux_done, base + (order["prep", g, 3] if more else order["madd1", g, 0]) + 1)
                for s in range(NS):
                    scores(pe, g, s, start, (0, 1))
                    if more:
                        max_unit(pe, s, 0)
                    scores(pe, g, s, start, (2, 3))
                    if more:
                        max_unit(pe, s, 1)
                    for k in YCHUNKS[s]:
                        if k % CH == 0:
                            wait(pe, ymul_done, EG * n + k // CH)
                            if first and g == 0 and k == 0:
                                pe.wait_ge(gT_done, 1)
                        pe.wait_ge(act_done, start + k + 1)
                        last_ = nc.tensor.matmul(yp[:, :], w2[:, NH * (g % 2) + k, :], hid[:, k, :],
                                                 start=(k % CH == 0), stop=(k % CH == CH - 1))
                        if k % CH == CH - 1:
                            last_.then_inc(y_done, 1)
                    if more:
                        max_unit(pe, s, 2)
                    if s:
                        values(pe, n, s - 1, g % 2)
                    if s == 5 and more:
                        o = order["madd0", g]
                        max_rows(pe, n + 1, 0, base + o, (par + o) % 2)
                    if s == 7:
                        o = order["ot0", g]
                        out_rows(pe, n, 0, base + o, (par + o) % 2)
                    if more:
                        max_unit(pe, s, 3)

        def prep_split(dve, m, u, parity, unit, bank):
            dve.wait_ge(aux_ready, unit + 1)
            dve.wait_ge(hic_done, 4 * m + u + 1)
            wait(dve, sc_ready, SC_UNITS * (m - 1))
            dst = (kT, qT)[u % 2][parity]
            nc.vector.scalar_tensor_tensor(out=dst[:, W * (u // 2):W * (u // 2) + W], in0=aux[bank][:, :],
                                           scalar=lo_row[u % 2], in1=hic[:, u % 2, :],
                                           op0=ALU.mult, op1=ALU.add).then_inc(aux_done, 1)

        def maximum(dve, s, h, unit, bank):
            i, _, cols, diagonal, slot = MAXES[s]
            dve.wait_ge(aux_ready, unit + 1)
            if not diagonal:
                nc.vector.reduce_max(maxes[:, i, slot, h:h + 1], aux[bank][:, 0:cols], axis=AX.X).then_inc(aux_done, 1)
                return
            wait(dve, aux_done, unit - 1)
            if cols > P:
                other = 1 if i < 4 else 2
                nc.vector.reduce_max(maxes[:, i, other, h:h + 1], aux[bank][:, 0:cols - P], axis=AX.X)
            elif not isinstance(unit, int):
                dve.sem_inc(dve_turn, 1)
            nc.vector.tensor_tensor_reduce(out=junk[:, bank, :], in0=aux[bank][:, cols - P:cols], in1=cmask,
                                           scale=1.0, scalar=LOW, op0=ALU.add, op1=ALU.max,
                                           accum_out=maxes[:, i, 0, h:h + 1]).then_inc(aux_done, 1)

        def spread_maxima(dve, m, c, unit):
            dst = mspread[:, :, :].rearrange("p t (h r) -> p t h r", r=32)
            dve.wait_ge(aux_done, unit + 1)
            nc.vector.reduce_max(mrow[:, :, :], maxes[:, 4 * c:4 * c + 4].rearrange("p t s h -> p t h s"),
                                 axis=AX.X).then_inc(mrow_done, 1)
            dve.wait_ge(mrow_done, 2 * m + c + 1)
            nc.vector.tensor_scalar(dst[:, :, :, 24].bitcast(F32R), mrow[:, :, :], -1.0, None, ALU.mult) \
                .then_inc(negh_done, 1)
            dve.wait_ge(negh_done, 2 * m + c + 1)
            nc.vector.scalar_tensor_tensor(out=dst[:, :, :, 25].bitcast(F32R), in0=mrow[:, :, :], scalar=-1.0,
                                           in1=dst[:, :, :, 24], op0=ALU.mult, op1=ALU.subtract).then_inc(msp_ready, 1)

        def add_max_rows(dve, c, parity, unit, bank):
            dst = qT[parity][:, W * c:W * c + W]
            dve.wait_ge(aux_ready, unit + 1)
            nc.vector.tensor_tensor(dst, aux[bank][:, :], dst.bitcast(F32), ALU.add).then_inc(aux_done, 1)

        def normalise(dve, n, g, c, unit, bank):
            src = aux[bank][:, :].rearrange("p (t h r) -> p t h r", h=HG, r=32)
            dve.wait_ge(aux_ready, unit + 1)
            nc.vector.reciprocal(rden[:, :, :], src[:, :, :, D]).then_inc(rden_done, 1)
            dve.wait_ge(rden_done, 2 * n + c + 1)
            nc.vector.tensor_tensor(attn[:, 4 * c:4 * c + 4, g], src[:, :, :, 0:D], bcast(rden[:, :, :], D),
                                    ALU.mult).then_inc(aux_done, 1)

        def finish(dve, b, what, c, unit, bank):
            dve.wait_ge(aux_ready, unit + 1)
            if what == "ft":
                nc.vector.tensor_copy(attnT[:, W * c:W * c + W], aux[bank][:, :]).then_inc(aux_done, 1)
            else:
                dve.wait_ge(xb_done, 2 * b)
                dst = xres[:, c]
                nc.vector.tensor_tensor(dst, aux[bank][:, :].rearrange("p (t c) -> p t c", c=C), dst,
                                        ALU.add).then_inc(aux_done, 1)

        def low_part(dve, r):
            dve.wait_ge(xT_ready, r + 1)
            dve.wait_ge(xh_done, r + 1)
            cols = slice(W * r, W * r + W)
            nc.vector.tensor_tensor(xl[:, cols], sc[r % 4][:, :], xh[:, cols].bitcast(F32),
                                    ALU.subtract).then_inc(xl_done, 1)

        def vector_batch(b, first, last):
            dve, order, base, par = nc.vector, aux_order(first, last), aux_base(b), aux_parity(b)
            for g in range(G4):
                n = G4 * b + g
                for k in sorted(AFTER):
                    what, u = AFTER[k]
                    if not present(what, g, first, last):
                        continue
                    o = order[what, g, u]
                    unit, bank = base + o, (par + o) % 2
                    if what == "madd1":
                        add_max_rows(dve, 1, g % 2, unit, bank)
                    elif what == "ot1":
                        normalise(dve, n - 1, (g - 1) % G4, 1, unit, bank)
                    elif what == "prep":
                        prep_split(dve, n + 1, u, (g + 1) % 2, unit, bank)
                    else:
                        finish(dve, b, what, u, unit, bank)
                more = present("prep", g, first, last)
                for s in range(NS):
                    for h in range(HG):
                        if h == HG - 1 and s == 5 and more:
                            o = order["madd0", g]
                            add_max_rows(dve, 0, (g + 1) % 2, base + o, (par + o) % 2)
                        if h == HG - 1 and s == 7:
                            o = order["ot0", g]
                            normalise(dve, n, g, 0, base + o, (par + o) % 2)
                        if more:
                            o = order["max", g, s, h]
                            maximum(dve, s, h, base + o, (par + o) % 2)
                    if more and s in (3, NS - 1):
                        spread_maxima(dve, n + 1, s // 4 // 2, base + o)
                    if s in YEND:
                        gate_expert(dve, b, g, n, YEND[s])

        def gate_expert(dve, b, g, n, i):
            e = EG * (g % 2) + i
            adds = (E - 1) * (2 * b + g // 2)
            dve.wait_ge(y_done, EG * n + i + 1)
            dve.wait_ge(gates_loaded, 16 * (n + 1))
            if e > 0:
                wait(dve, yadd_done, adds + (e - 2 if e > 2 else 0))
            dst = yT[:, W * (g // 2):W * (g // 2) + W] if e == 0 else ytmp[:, e % 2, :]
            nc.vector.scalar_tensor_tensor(out=dst.rearrange("p (t q) -> p t q", q=P),
                                           in0=yp[:, :].rearrange("p (t q) -> p t q", q=P),
                                           scalar=b2T[:, e:e + 1], in1=gates[:, :, i, :],
                                           op0=ALU.add, op1=ALU.mult).then_inc(ymul_done, 1)

        @block.sync
        def _(sp):
            for i in range(4):
                sp.dma_start(x_in[:, 8 * i:8 * i + 8, :].rearrange("p (n i) c -> p n i c", i=4),
                             x_v[2 * i:2 * i + 2].rearrange("n p i c -> p n i c")).then_inc(x_loaded[i], 16)
            sp.dma_start(wqkv[:, :], w_qkv).then_inc(w_loaded, 16)
            sp.dma_start(w1_in, W1.rearrange("e h i -> h e i")).then_inc(w1_loaded, 16)
            sp.dma_start(w2[:, :, :], W2.rearrange("e (c p) h -> p (e c) h", p=P)).then_inc(w2_loaded, 16)
            sp.dma_start(wp[:, :], w_proj).then_inc(p_loaded, 16)
            sp.dma_start(bp[:, :], b_proj.partition_broadcast(P)).then_inc(p_loaded, 16)
            for n in range(B):
                sp.wait_ge(vg_done, 4 * (n + 1))
                sp.dma_start(v_scr[G4 * n:G4 * n + G4].rearrange("g p f -> p g f"),
                             v_all[:, n].rearrange("p g t c -> p g (t c)")).then_inc(v_stored, 16)
            sp.wait_ge(v_stored, 16 * B)
            load_v(sp, 0)
            sp.wait_ge(gT_done, 1)
            for k in range(2):
                sp.dma_start(g_scr[16 * k:16 * k + 16].rearrange("t (e p) -> (t e) p", p=P),
                             grow[:, k, :]).then_inc(g_stored, 16)
            sp.wait_ge(g_stored, 32)
            load_gates(sp, 0, 0)
            over_batches(sp, sync_batch)
            tail = aux_base(B - 1) + len(aux_order(False, True))
            load_xres(sp, B)
            for c in range(2):
                sp.wait_ge(aux_done, tail + 4 + c)
                store(sp, B, c)
            sp.wait_ge(stored, 32 * B)

        @block.gpsimd
        def _(pool):
            nc.gpsimd.memset(small[:, :], 0.0).then_inc(small_zero, 1)
            nc.gpsimd.memset(half[:, :], -0.5).then_inc(pchain, 1)
            for i in range(2):
                nc.gpsimd.memset(v[i][:, :, :, :], 0.0).then_inc(zeroed, 1)
            nc.gpsimd.memset(mspread[:, :, :], 0.0).then_inc(zeroed, 1)
            for i in range(4):
                t = slice(8 * i, 8 * i + 8)
                pool.wait_ge(mv_ready, i + 1)
                nc.gpsimd.tensor_scalar(veps[:, t], meanvar[:, t, 1], EPS, None, ALU.add).then_inc(pchain, 1)
                pool.wait_ge(pchain, 2 + i)
                nc.gpsimd.tensor_tensor(rstd[:, t], veps[:, t], half[:, t], ALU.pow).then_inc(rstd_ready, 1)
            pool.wait_ge(zeroed, 3)
            for i in range(2):
                nc.gpsimd.memset(v[i][:, :, :, D:D + 1], 1.0).then_inc(zeroed, 1)
            expand_v(pool, 0, 0)
            over_batches(pool, pool_batch)
            finish_bias(pool, B)

        @block.scalar
        def _(act):
            act.dma_start(cst[:, :], consts).then_inc(c_loaded, 16)
            act.wait_ge(small_zero, 1)
            act.dma_start(small[0:32, :], b1.rearrange("e (c p) -> (e c) p", p=P)).then_inc(s_loaded, 16)
            act.dma_start(small[32:40, :], b2).then_inc(s_loaded, 16)
            act.dma_start(small[64:72, :], Wg).then_inc(s_loaded, 16)
            for r in range(8):
                act.wait_ge(xT_ready, r + 1)
                nc.scalar.copy(xh[:, W * r:W * (r + 1)], sc[r % 4][:, :]).then_inc(xh_done, 1)
            for u in range(4):
                prep_hic(act, u, u, u % 2, u - 2)
            act.wait_ge(w1_loaded, 16)
            for i in range(2):
                nc.scalar.copy(w1h[:, 4 * i:4 * i + 4, :], w1_in[:, 4 * i:4 * i + 4, :]).then_inc(w1h_done, 1)
            for r in range(NT // 2):
                act.wait_ge(vg_ready, r + 1)
                src = sc[r % 4][:, 0:2 * (C + E)].rearrange("p (t n) -> p t n", t=2)
                n, t = divmod(2 * r, TPB)
                nc.scalar.copy(v_all[:, n, :, t:t + 2, :].rearrange("p g t c -> p t g c"),
                               src[:, :, 0:C].rearrange("p t (g c) -> p t g c", c=32))
                nc.scalar.copy(logits[:, 2 * r:2 * r + 2, :], src[:, :, C:C + E]).then_inc(vg_done, 1)
            act.wait_ge(dlt_ready, 1)
            nc.scalar.activation(ex, dlt, ACT.Exp).then_inc(ex_ready, 1)
            act.wait_ge(v_stored, 16 * B)
            over_batches(act, act_batch)
            evacuate_ov(act, G4 * B - 1, 1)

        @block.tensor
        def _(pe):
            pe.wait_ge(c_loaded, 16)
            pe.wait_ge(s_loaded, 48)
            nc.tensor.transpose(ov[:, 0:P], small[:, :], ident).then_inc(smallT_ready, 1)
            for r in range(8):
                pe.wait_ge(xn_ready, r + 1)
                wait(pe, xl_done, r - 3)
                for t in range(4):
                    last_ = nc.tensor.transpose(sc[r % 4][:, P * t:P * t + P], x_in[:, 4 * r + t, :], ident)
                last_.then_inc(xT_ready, 1)
            pe.wait_ge(wkq_ready, 1)
            pe.wait_ge(xl_done, 8)
            for u in range(4):
                prep_product(pe, 0, u, u, u % 2, 0)
            pe.wait_ge(wvg_ready, 1)
            pe.wait_ge(aux_done, 4)
            unit = 4
            for s in range(NS):
                for h in range(HG):
                    max_scores(pe, s, h, 0, unit, unit % 2)
                    unit += 1
                for r in YCHUNKS[s]:
                    wait(pe, vg_done, r - 3)
                    for t in range(2):
                        tok = slice(P * (2 * r + t), P * (2 * r + t) + P)
                        dst = sc[r % 4][:, (C + E) * t:(C + E) * (t + 1)]
                        nc.tensor.matmul(dst, xh[:, tok], wvgh[:, :], start=True, stop=False)
                        nc.tensor.matmul(dst, xh[:, tok], wvgl[:, :], start=False, stop=False)
                        last_ = nc.tensor.matmul(dst, xl[:, tok], wvgh[:, :], start=False, stop=True)
                    last_.then_inc(vg_ready, 1)
                if s == 5:
                    max_rows(pe, 0, 0, unit, unit % 2)
                    unit += 1
            pe.wait_ge(g_ready, 1)
            for k in range(2):
                last_ = nc.tensor.transpose(yp[:, P * k:P * k + P],
                                            g_all[:, 16 * k:16 * k + 16, :].rearrange("p t e -> p (t e)"), ident)
            last_.then_inc(gT_ready, 1)
            pe.wait_ge(w1h_done, 2)
            pe.wait_ge(w1l_done, 1)
            pe.wait_ge(vg_done, NT // 2)
            over_batches(pe, tensor_batch)
            n, unit = G4 * B - 1, aux_base(B - 1) + len(aux_order(False, True))
            values(pe, n, NS - 1, n % 2)
            out_rows(pe, n, 1, unit, unit % 2)
            for c in range(2):
                attn_columns(pe, c, unit + 1 + c, (unit + 1 + c) % 2, unit)
            for c in range(2):
                project(pe, B, c, unit + 3 + c, (unit + 3 + c) % 2, unit + 1 + c)

        @block.vector
        def _(dve):
            links = [0]

            def link(ins):
                links[0] += 1
                ins.then_inc(chain, 1)
                dve.wait_ge(chain, links[0])

            nc.vector.memset(maxes[:, :, :, :], LOW)
            link(nc.vector.memset(wkq[:, :, :, :], 0.0))
            dve.wait_ge(w_loaded, 16)
            heads = wkq[:, :, :, :].rearrange("p a g (h r) -> p a (g h) r", r=32)
            for kq, (col, scale) in enumerate(((C, 1.0), (0, SCALE))):
                src = wqkv[:, col:col + C].rearrange("p (h d) -> p h d", d=D).unsqueeze(2).to_broadcast([P, H, 3, D])
                link(nc.vector.tensor_scalar(heads[:, kq, :, 0:3 * D].rearrange("p h (a d) -> p h a d", d=D), src,
                                             scale, None, ALU.mult))
            link(nc.vector.tensor_copy(wkqh[:, :, :, :], wkq[:, :, :, :]))
            nc.vector.tensor_tensor(wkql[:, :, :, :], wkq[:, :, :, :], wkqh[:, :, :, :].bitcast(F32),
                                    ALU.subtract).then_inc(wkq_ready, 1)
            for i in range(4):
                dve.wait_ge(x_loaded[i], 16)
                for t in range(8 * i, 8 * i + 8):
                    last_ = nc.vector.bn_stats(stats[:, t, :], x_in[:, t, :])
                link(last_)
                for t in range(8 * i, 8 * i + 8):
                    last_ = nc.vector.bn_aggr(meanvar[:, t, :], stats[:, t, :])
                last_.then_inc(mv_ready, 1)
            dve.wait_ge(mv_ready, 4)
            for r in range(8):
                dve.wait_ge(rstd_ready, r // 2 + 1)
                for t in range(4 * r, 4 * r + 4):
                    last_ = nc.vector.tensor_scalar(x_in[:, t, :], x_in[:, t, :], meanvar[:, t, 0:1], rstd[:, t:t + 1],
                                                    ALU.subtract, ALU.mult)
                last_.then_inc(xn_ready, 1)
                if r:
                    low_part(dve, r - 1)
            low_part(dve, 7)
            dve.wait_ge(c_loaded, 16)
            for u in range(4):
                prep_split(dve, 0, u, 0, u, u % 2)
            dve.wait_ge(smallT_ready, 1)
            link(nc.vector.tensor_copy(smallT[:, :], ov[:, 0:72]))
            nc.vector.tensor_copy(wvg[:, 0:C], wqkv[:, 2 * C:3 * C])
            link(nc.vector.tensor_copy(wvg[:, C:C + E], wgT))
            link(nc.vector.tensor_copy(wvgh[:, :], wvg[:, :]))
            nc.vector.tensor_tensor(wvgl[:, :], wvg[:, :], wvgh[:, :].bitcast(F32), ALU.subtract).then_inc(wvg_ready, 1)
            unit = 4
            for s in range(NS):
                for h in range(HG):
                    maximum(dve, s, h, unit, unit % 2)
                    unit += 1
                if s == 3:
                    spread_maxima(dve, 0, 0, unit - 1)
                if s == 5:
                    add_max_rows(dve, 0, 0, unit, unit % 2)
                    unit += 1
                if s == 6:
                    dve.wait_ge(w1h_done, 2)
                    nc.vector.tensor_tensor(w1l[:, :, :], w1_in, w1h[:, :, :].bitcast(F32),
                                            ALU.subtract).then_inc(w1l_done, 1)
            spread_maxima(dve, 0, 1, unit - 1)

            dve.wait_ge(vg_done, NT // 2)

            def one_hot(dst, values_, top, rank):
                link(nc.vector.reduce_max(top, values_, axis=AX.X))
                link(nc.vector.tensor_tensor(eq, values_, bcast(top, E), ALU.is_equal))
                link(nc.vector.tensor_tensor(eq, eq, rank8.unsqueeze(1).to_broadcast([P, NT, E]), ALU.mult))
                link(nc.vector.reduce_max(rank, eq, axis=AX.X))
                link(nc.vector.tensor_tensor(dst, eq, bcast(rank, E), ALU.is_equal))

            one_hot(first1, logits, top1, c1)
            link(nc.vector.scalar_tensor_tensor(out=rest, in0=first1, scalar=LOW, in1=logits,
                                                op0=ALU.mult, op1=ALU.add))
            one_hot(first2, rest, top2, c2)
            nc.vector.tensor_tensor(dlt, top2, top1, ALU.subtract).then_inc(dlt_ready, 1)
            dve.wait_ge(ex_ready, 1)
            link(nc.vector.tensor_scalar(den, ex, 1.0, None, ALU.add))
            link(nc.vector.reciprocal(r1, den))
            link(nc.vector.tensor_tensor(r2, ex, r1, ALU.mult))
            link(nc.vector.tensor_tensor(first1, first1, bcast(r1, E), ALU.mult))
            link(nc.vector.tensor_tensor(first2, first2, bcast(r2, E), ALU.mult))
            nc.vector.tensor_tensor(g_all, first1, first2, ALU.add).then_inc(g_ready, 1)
            dve.wait_ge(gT_ready, 1)
            nc.vector.tensor_copy(grow, yp[:, 0:2 * P].rearrange("p (k q) -> p k q", k=2)).then_inc(gT_done, 1)
            over_batches(dve, vector_batch)
            n, unit = G4 * B - 1, aux_base(B - 1) + len(aux_order(False, True))
            normalise(dve, n, G4 - 1, 1, unit, unit % 2)
            for i, (what, c) in enumerate((("ft", 0), ("ft", 1), ("fo", 0), ("fo", 1))):
                finish(dve, B, what, c, unit + 1 + i, (unit + 1 + i) % 2)


_INS = ["L0_attn_x", "L0_attn_w_qkv", "L0_attn_w_proj", "L0_attn_b_proj", "L0_ffn_Wg", "L0_ffn_W1", "L0_ffn_b1",
        "L0_ffn_W2", "L0_ffn_b2"]


def shape_constants():
    c = np.zeros((P, CONSTS), np.float32)
    c[:, 0:P] = np.eye(P)
    c[:, P:2 * P] = np.triu(np.full((P, P), MASKED), 1)
    row = np.arange(P) % 32
    for kq, lo in enumerate((D, 2 * D)):
        low = (row >= lo) & (row < lo + D)
        c[:, 2 * P + 2 * kq] = low
        c[:, 2 * P + 2 * kq + 1] = 1 - 2 * low
    c[:, 2 * P + 4] = (row == 3 * D) | (row == 3 * D + 1)
    c[:, 2 * P + 6:] = np.arange(E, 0, -1)
    return c


def kernel(**inputs):
    import concourse.bacc as bacc
    from concourse.bass_utils import run_bass_kernel_spmd

    nc = bacc.Bacc("TRN2", target_bir_lowering=False, num_devices=1)
    arrays, args = {}, []
    for name in _INS:
        a = np.ascontiguousarray(inputs[name])
        arrays[f"in_{name}"] = a
        args.append(nc.dram_tensor(f"in_{name}", a.shape, mybir.dt.from_np(a.dtype), kind="ExternalInput").ap())
    arrays["shape_consts"] = shape_constants()
    args.append(nc.dram_tensor("shape_consts", (P, CONSTS), F32, kind="ExternalInput").ap())
    args.append(nc.dram_tensor("out_0", (B, T, C), F32, kind="ExternalOutput").ap())
    layer_kernel(nc, *args)
    r = run_bass_kernel_spmd(nc, [arrays], core_ids=[0])
    return r.results[0]["out_0"]
```

```python
from contextlib import ExitStack

import concourse.bass as bass
import numpy as np
from concourse import mybir

F32 = mybir.dt.float32
F32R = mybir.dt.float32r
ACT = mybir.ActivationFunctionType
ALU = mybir.AluOpType
AX = mybir.AxisListType

B, T, C = 4, 1024, 128
TOK = B * T
P = 128
NT = TOK // P
TPB = T // P
H, D = 16, 8
HG = 4
G4 = H // HG
E, I = 8, 512
CH = I // P
EG = 4
NH = EG * CH
W = 512
EPS = 1e-5
SCALE = float(D) ** -0.5
CONSTS = 2 * P + 6 + E
LOW = -3.0e38
MASKED = -1.0e30

SUB = [(0, j, P * j, W - P * j) for j in range(4)] + [(1, j, W, W) for j in range(4)] + \
      [(1, j, P * j, T - P * j) for j in range(4, TPB)]
NS = len(SUB)
DIAG = [s for s, (c, j, q, n) in enumerate(SUB) if q == P * j]
MAXES = [(i, 0, P * (i + 1), True, 0) for i in range(4)] + \
        [x for i in range(4, TPB) for x in ((i, 0, W, False, 1), (i, W, P * (i + 1) - W, True, 0))]
ORDER = "MXSSMYMSMSGV"
EXTRA = {5: "madd0", 7: "ot0"}
YCHUNKS = [[0, 1, 2], [3], [4], [5], [6, 7], [8], [9], [10], [11], [12], [13], [14, 15]]
YEND = {s: x[-1] // CH for s, x in enumerate(YCHUNKS) if x[-1] % CH == CH - 1}
AFTER_K = [2, 3, 4, 5, 6, 7, 9, 10, 12, 13]
AFTER = dict(zip(AFTER_K, (("madd1", 0), ("ot1", 0), ("prep", 0), ("ft", 0), ("prep", 1), ("ft", 1), ("prep", 2),
                           ("prep", 3), ("fo", 0), ("fo", 1))))
FIRST_AFTER = {13: ("madd1", 0)}

VG_UNIT = [1, 2, 3, 4, 5, 7, 8, 9, 11, 12, 16, 17, 18, 19, 21, 23]
LN_UNIT = [1, 4, 5, 6, 6, 7, 8, 11, 12, 13, 13, 14]
LN_PARTS = [part for i in (2, 3) for part in (
    ("stats", i), ("norm", i),
    ("xt", 2 * i), ("xt", 2 * i + 1),
    ("low", 2 * i), ("low", 2 * i + 1))]
HID_UNIT = [23, 23, 23, 23, 25, 25, 28, 29, 30, 36, 38, 40]
EARLY = len(HID_UNIT)
GATES_UNIT = [23, 28, 31]
NEXT_UNIT = [32, 33, 35, 39]
PARTS = [(7, ("prep", 2)), (7, ("prep", 3)), (HG * 6 - 1, ("madd", 0))] + \
        list(zip(NEXT_UNIT, [("next", u) for u in range(4)])) + \
        [(m + 1, ("next_split", u)) for u, m in enumerate(NEXT_UNIT)] + \
        list(zip(GATES_UNIT, [("top_two", 0), ("weigh", 0), ("turn_gates", 0)])) + \
        list(zip(VG_UNIT, [("vg", r) for r in range(NT // 2)])) + list(zip(LN_UNIT, LN_PARTS)) + \
        list(zip(HID_UNIT, [("hid", k) for k in range(EARLY)]))
SETUP = [("prep", 0), ("xt", 2), ("prep", 1), ("xt", 3), ("low", 2), ("low", 3)] + \
        [part for m in range(HG * NS) for part in [("max", m)] + [p for at, p in PARTS if at == m]]
SIDE = [("xt", 0), ("xt", 1)] + [x for x in SETUP if x[0] in ("xt", "vg")]
SIDE_BANK = {x: i % 2 for i, x in enumerate(SIDE)}
SIDE_BEFORE = {x: SIDE[i] for i, x in enumerate(SIDE[2:])}
SETUP_AUX = {x: i for i, x in enumerate(x for x in SETUP if x[0] in ("prep", "max", "madd"))}
AUX_START = len(SETUP_AUX)
SC_UNITS = NH + HG * NS


def after(g, first):
    return FIRST_AFTER if first and g == 0 else AFTER


def present(what, g, first, last):
    if what == "prep":
        return not (last and g == G4 - 1) and not (first and g == 0)
    if what == "next":
        return not (last and g == G4 - 1)
    if what == "ot1":
        return not (first and g == 0)
    if what in ("ft", "fo"):
        return g == 0 and not first
    return True


def aux_order(first, last):
    names = []
    for g in range(G4):
        for k in sorted(after(g, first)):
            what, u = after(g, first)[k]
            if present(what, g, first, last):
                names.append((what, g, u))
        for s in range(NS):
            more = present("next", g, first, last)
            maxima = iter(range(HG))
            for part in ORDER:
                if part == "M" and more:
                    names.append(("max", g, s, next(maxima)))
                if part == "X" and s in EXTRA and (more or EXTRA[s] != "madd0"):
                    names.append((EXTRA[s], g))
    return {name: i for i, name in enumerate(names)}


def aux_base(b):
    if isinstance(b, int) and b == 0:
        return AUX_START
    whole = len(aux_order(False, False))
    return b * whole + (AUX_START + len(aux_order(True, False)) - whole)


def aux_parity(b):
    return aux_base(b if isinstance(b, int) else 1) % 2


def wait(eng, sem, value):
    if not isinstance(value, int) or value > 0:
        eng.wait_ge(sem, value)


def bcast(ap, n):
    return ap.unsqueeze(len(ap.shape)).to_broadcast([*ap.shape, n])


def layer_kernel(nc, x, w_qkv, w_proj, b_proj, Wg, W1, b1, W2, b2, consts, out):
    ctx = ExitStack()
    with ctx:
        def sb(name, shape, dt=F32):
            return ctx.enter_context(nc.sbuf_tensor(name, shape, dt))

        def sem(name):
            return ctx.enter_context(nc.semaphore(name))

        cst = sb("cst", [P, CONSTS])
        ident, cmask = cst[:, 0:P], cst[:, P:2 * P]
        lo_row = [cst[:, 2 * P + 2 * kq:2 * P + 2 * kq + 1] for kq in range(2)]
        hi_sign = [cst[:, 2 * P + 2 * kq + 1:2 * P + 2 * kq + 2] for kq in range(2)]
        ones_row = [cst[:, 2 * P + 4 + kq:2 * P + 5 + kq] for kq in range(2)]
        w1h, w1l = sb("w1h", [P, E, I], F32R), sb("w1l", [P, E, I], F32R)
        w2 = sb("w2", [P, E * CH, C])
        wkqh, wkql = sb("wkqh", [P, 2, G4, P], F32R), sb("wkql", [P, 2, G4, P], F32R)
        wvgh, wvgl = sb("wvgh", [P, C + E], F32R), sb("wvgl", [P, C + E], F32R)
        wvg = sb("wvg", [P, C + E])
        wqkv = sb("wqkv", [P, 3 * C])
        wp, bp = sb("wp", [P, C]), sb("bp", [P, C])
        small = sb("small", [P, P])
        smallT = sb("smallT", [P, 72])
        b1T, b2T, wgT = smallT[:, 0:32], smallT[:, 32:40], smallT[:, 64:72]
        xh, xl = sb("xh", [P, TOK], F32R), sb("xl", [P, TOK], F32R)
        kT = [sb(f"kT{i}", [P, T], F32R) for i in range(2)]
        qT = [sb(f"qT{i}", [P, T], F32R) for i in range(2)]
        v = [sb(f"v{i}", [P, TPB, HG, 32]) for i in range(2)]
        hic = sb("hic", [P, 2, W])
        vst = sb("vst", [P, TPB, 32])
        probs = sb("probs", [P, 2, HG, W])
        maxes = sb("maxes", [P, TPB, 3, HG])
        mrow = sb("mrow", [P, 4, HG])
        mspread = sb("mspread", [P, 4, P])
        junk = sb("junk", [P, 2, P])
        ot = sb("ot", [P, 2, W])
        rden = sb("rden", [P, 4, HG])
        attn = sb("attn", [P, TPB, G4, HG, D])
        attnT = sb("attnT", [P, T])
        hid = sb("hid", [P, NH, W])
        gates = sb("gates", [P, 4, EG, P])
        ytmp = sb("ytmp", [P, 2, W])
        yT = sb("yT", [P, T])
        xres = sb("xres", [P, 2, 4, C])
        x_in = hid[:, 8:16, :].rearrange("p a (b c) -> p (a b) c", c=C)
        w1_in = hid[:, 0:8, :]
        wkq = ytmp[:, :, :].rearrange("p a (g r) -> p a g r", r=P)
        v_all = probs[:, :, :, :].rearrange("p a b w -> p (a b w)") \
            .rearrange("p (n g t c) -> p n g t c", n=B, g=G4, c=32)
        stats = attnT[:, 0:NT * 6].rearrange("p (t s) -> p t s", s=6)
        meanvar = attnT[:, NT * 6:NT * 8].rearrange("p (t s) -> p t s", s=2)
        rstd = attnT[:, NT * 8:NT * 9]
        veps = attnT[:, NT * 9:NT * 10]
        half = attnT[:, NT * 10:NT * 11]
        gt = gates[:, :, :, :].rearrange("p t e q -> p (t e q)")

        def gtile(i):
            return gt[:, i * NT * E:(i + 1) * NT * E].rearrange("p (t e) -> p t e", e=E)

        logits, eq, first1, rest, first2 = (gtile(i) for i in range(5))
        grow = ot[:, 0, 0:2 * P].rearrange("p (k q) -> p k q", k=2)
        g_all = ytmp[:, 1, 0:NT * E].rearrange("p (t e) -> p t e", e=E)
        gcol = attn[:, :, :, :, :].rearrange("p a b c d -> p (a b c d)")
        rank8 = cst[:, 2 * P + 6:2 * P + 6 + E]
        top1, top2, c1, c2, dlt, ex, den, r1, r2 = (gcol[:, 32 + 32 * i:64 + 32 * i] for i in range(9))

        sc = [ctx.enter_context(nc.psum_tensor(f"sc{i}", [P, W], F32)) for i in range(4)]
        aux = [ctx.enter_context(nc.psum_tensor(f"aux{i}", [P, W], F32)) for i in range(2)]
        ov = ctx.enter_context(nc.psum_tensor("ov", [P, W], F32))
        yp = ctx.enter_context(nc.psum_tensor("yp", [P, W], F32))

        v_scr = nc.dram_tensor("v_scr", [B * G4, P, TPB * 32], F32, kind="Internal").ap()
        g_scr = nc.dram_tensor("g_scr", [NT, E * P], F32, kind="Internal").ap()
        x_v = x.rearrange("b (n i p) c -> (b n) p i c", i=4, p=P)
        out_v = out.rearrange("b (n i p) c -> (b n) p i c", i=4, p=P)

        x_loaded = [sem(f"x_loaded{i}") for i in range(4)]
        c_loaded, s_loaded, w_loaded = sem("c_loaded"), sem("s_loaded"), sem("w_loaded")
        w1_loaded, w2_loaded, p_loaded = sem("w1_loaded"), sem("w2_loaded"), sem("p_loaded")
        chain = sem("chain")
        pchain = sem("pchain")
        small_zero, smallT_ready, smallT_done = sem("small_zero"), sem("smallT_ready"), sem("smallT_done")
        mv_ready, rstd_ready, xn_ready = sem("mv_ready"), sem("rstd_ready"), sem("xn_ready")
        xT_ready, xh_done, xl_done = sem("xT_ready"), sem("xh_done"), sem("xl_done")
        wkq_zero, wkq_laid, wkqh_done, wkq_ready, wvg_ready, w1h_done, w1l_done = sem("wkq_zero"), sem("wkq_laid"), sem("wkqh_done"), sem("wkq_ready"), sem("wvg_ready"), sem("w1h_done"), sem("w1l_done")
        vg_ready, vg_done, v_stored = sem("vg_ready"), sem("vg_done"), sem("v_stored")
        dlt_ready, ex_ready, g_ready, gT_ready, gT_done, g_stored = (
            sem(n) for n in ("dlt_ready", "ex_ready", "g_ready", "gT_ready", "gT_done", "g_stored"))
        zeroed = sem("zeroed")
        next_ready, next_done = sem("next_ready"), sem("next_done")
        sc_ready, act_done = sem("sc_ready"), sem("act_done")
        aux_ready, aux_done = sem("aux_ready"), sem("aux_done")
        hic_done = sem("hic_done")
        mrow_done, negh_done, msp_ready = sem("mrow_done"), sem("negh_done"), sem("msp_ready")
        sel_done, pv_done, ot_evac, rden_done = sem("sel_done"), sem("pv_done"), sem("ot_evac"), sem("rden_done")
        vst_loaded, v_done = sem("vst_loaded"), sem("v_done")
        y_done, ymul_done, yadd_done, gates_loaded = sem("y_done"), sem("ymul_done"), sem("yadd_done"), sem("gates_loaded")
        xres_loaded, xb_done, stored = sem("xres_loaded"), sem("xb_done"), sem("stored")

        dve_turn, pool_turn = sem("dve_turn"), sem("pool_turn")
        block = ctx.enter_context(nc.Block())

        def over_batches(eng, body):
            body(0, True, False)
            with eng.Fori(1, B - 1) as b:
                body(b, False, False)
            body(B - 1, False, True)

        def load_v(sp, n):
            sp.dma_start(vst[:, :, :].rearrange("p t c -> p (t c)"),
                         v_scr[bass.ds(n, 1)].rearrange("o p f -> p (o f)")).then_inc(vst_loaded, 16)

        def load_gates(sp, b, g):
            e0 = EG * (g % 2)
            sp.dma_start(gates[:, :, :, :].rearrange("p t e q -> p t (e q)"),
                         g_scr[bass.ds(b * TPB + g // 2 * 4, 4), e0 * P:(e0 + EG) * P].partition_broadcast(P)) \
                .then_inc(gates_loaded, 16)

        def load_xres(sp, b):
            for c in range(2):
                sp.dma_start(xres[:, c], x_v[bass.ds(2 * b - 2 + c, 1)].rearrange("o p i c -> p (o i) c")) \
                    .then_inc(xres_loaded, 16)

        def store(sp, b, c):
            sp.dma_start(out_v[bass.ds(2 * b - 2 + c, 1)].rearrange("o p i c -> p (o i) c"), xres[:, c]) \
                .then_inc(stored, 16)

        def sync_batch(b, first, last):
            sp, order, base = nc.sync, aux_order(first, last), aux_base(b)
            for g in range(G4):
                n = G4 * b + g
                if g == 0 and not first:
                    wait(sp, stored, 32 * b - 32)
                    load_xres(sp, b)
                if present("next", g, first, last):
                    sp.wait_ge(v_done, n + 1)
                    load_v(sp, n + 1)
                if g == 0 and not first:
                    for c in range(2):
                        sp.wait_ge(aux_done, base + order["fo", 0, c] + 1)
                        store(sp, b, c)
                if present("next", g, first, last):
                    sp.wait_ge(ymul_done, EG * n + EG)
                    load_gates(sp, b + (g + 1) // G4, (g + 1) % G4)

        def expand_v(pool, n, parity):
            pool.wait_ge(zeroed, 5)
            pool.wait_ge(vst_loaded, 16 * (n + 1))
            wait(pool, pv_done, NS * (n - 1))
            if not isinstance(n, int):
                pool.sem_inc(pool_turn, 1)
            nc.gpsimd.tensor_copy(v[parity][:, :, :, 0:D],
                                  vst[:, :, :].rearrange("p t (h d) -> p t h d", d=D)).then_inc(v_done, 1)

        def finish_bias(pool, b):
            pool.wait_ge(xres_loaded, 32 * b)
            wait(pool, p_loaded, 32)
            for c in range(2):
                nc.gpsimd.tensor_tensor(xres[:, c], xres[:, c],
                                        bp[:, :].unsqueeze(1).to_broadcast([P, 4, C]), ALU.add).then_inc(xb_done, 1)

        def pool_batch(b, first, last):
            pool = nc.gpsimd
            for g in range(G4):
                n = G4 * b + g
                if present("next", g, first, last):
                    expand_v(pool, n + 1, (g + 1) % 2)
                if g == 0 and not first:
                    finish_bias(pool, b)
                for s in range(NS):
                    if s in DIAG:
                        pool.wait_ge(act_done, SC_UNITS * n + NH + HG * (s + 1))
                        if not isinstance(n, int):
                            pool.sem_inc(pool_turn, 1)
                        block_ = probs[:, s % 2, :, 0:P]
                        nc.gpsimd.affine_select(out=block_, in_=block_, compare_op=ALU.is_ge, fill=0.0, base=0,
                                                pattern=[[0, HG], [1, P]], channel_multiplier=-1).then_inc(sel_done, 1)
                    if s in YEND:
                        e = EG * (g % 2) + YEND[s]
                        if e > 0:
                            half_ = yT[:, W * (g // 2):W * (g // 2 + 1)]
                            adds = (E - 1) * (2 * b + g // 2) + e - 1
                            pool.wait_ge(ymul_done, EG * n + YEND[s] + 1)
                            wait(pool, yadd_done, adds)
                            nc.gpsimd.tensor_tensor(half_, half_, ytmp[:, e % 2, :], ALU.add).then_inc(yadd_done, 1)

        def prep_hic(act, u, unit, bank, before):
            act.wait_ge(aux_ready, unit + 1)
            if u >= 2:
                act.wait_ge(aux_done, before + 1)
            nc.scalar.activation(hic[:, u % 2, :].bitcast(F32R), aux[bank][:, :], ACT.Identity,
                                 bias=ones_row[u % 2], scale=hi_sign[u % 2]).then_inc(hic_done, 1)

        def gelu(act, g, k, start):
            act.wait_ge(sc_ready, start + k + 1)
            nc.scalar.activation(hid[:, k, :], sc[k % 4][:, :], ACT.Gelu,
                                 bias=b1T[:, NH * (g % 2) + k:NH * (g % 2) + k + 1]).then_inc(act_done, 1)

        def evacuate_ov(act, n, c):
            act.wait_ge(pv_done, NS * n + (4 if c == 0 else NS))
            wait(act, rden_done, 2 * n + c - 1)
            nc.scalar.copy(ot[:, c, :], ov[:, :]).then_inc(ot_evac, 1)

        def act_batch(b, first, last):
            act, order, base = nc.scalar, aux_order(first, last), aux_base(b)
            for g in range(G4):
                n = G4 * b + g
                start = SC_UNITS * n
                wait(act, y_done, EG * n)
                for k in range(NH):
                    if not (first and g == 0 and k < EARLY):
                        gelu(act, g, k, start)
                    if k == 1 and not (first and g == 0):
                        evacuate_ov(act, n - 1, 1)
                    what, u = after(g, first).get(k, (None, 0))
                    if what == "prep" and present(what, g, first, last):
                        o = order[what, g, u]
                        prep_hic(act, u, base + o, (aux_parity(b) + o) % 2,
                                 base + order[what, g, max(u - 2, 0)])
                for s, (_, _, _, cols) in enumerate(SUB):
                    wait(act, pv_done, NS * n + s - 1)
                    for h in range(HG):
                        k = NH + HG * s + h
                        act.wait_ge(sc_ready, start + k + 1)
                        nc.scalar.activation(probs[:, s % 2, h, 0:cols], sc[k % 4][:, 0:cols],
                                             ACT.Exp).then_inc(act_done, 1)
                    if s == 4:
                        if first and g == 0:
                            act.wait_ge(g_stored, 32)
                        evacuate_ov(act, n, 0)

        def split_product(out_, wh, wl, mh, ml):
            nc.tensor.matmul(out_, wh, mh, start=True, stop=False)
            nc.tensor.matmul(out_, wh, ml, start=False, stop=False)
            return nc.tensor.matmul(out_, wl, mh, start=False, stop=True)

        def aux_free(pe, unit):
            wait(pe, aux_done, unit - 1)

        def prep_product(pe, g, u, unit, bank, token):
            aux_free(pe, unit)
            tok = bass.ds(token + W * (u // 2), W)
            split_product(aux[bank][:, :], wkqh[:, u % 2, g, :], wkql[:, u % 2, g, :],
                          xh[:, tok], xl[:, tok]).then_inc(aux_ready, 1)

        def hidden(pe, g, token, k, start):
            e, ch = EG * (g % 2) + k // CH, k % CH
            wait(pe, act_done, start + k - 3)
            split_product(sc[k % 4][:, :], w1h[:, e, P * ch:P * ch + P], w1l[:, e, P * ch:P * ch + P],
                          xh[:, bass.ds(token, W)], xl[:, bass.ds(token, W)]).then_inc(sc_ready, 1)

        def max_scores(pe, s, h, parity, unit, bank):
            i, k0, cols, _, _ = MAXES[s]
            rows = slice(32 * h, 32 * h + 32)
            aux_free(pe, unit)
            nc.tensor.matmul(aux[bank][:, 0:cols], qT[parity][rows, P * i:P * i + P],
                             kT[parity][rows, k0:k0 + cols], start=True, stop=True).then_inc(aux_ready, 1)

        def scores(pe, g, s, start, h):
            _, j, q, cols = SUB[s]
            k = NH + HG * s + h
            rows = slice(32 * h, 32 * h + 32)
            wait(pe, act_done, start + k - 3)
            nc.tensor.matmul(sc[k % 4][:, 0:cols], kT[g % 2][rows, P * j:P * j + P],
                             qT[g % 2][rows, q:q + cols], start=True, stop=True).then_inc(sc_ready, 1)

        def output_layer(pe, g, s, n, start, first):
            for k in YCHUNKS[s]:
                if k % CH == 0:
                    wait(pe, ymul_done, EG * n + k // CH)
                    if first and g == 0 and k == 0:
                        pe.wait_ge(gT_done, 1)
                pe.wait_ge(act_done, start + k + 1)
                last_ = nc.tensor.matmul(yp[:, :], w2[:, NH * (g % 2) + k, :], hid[:, k, :],
                                         start=(k % CH == 0), stop=(k % CH == CH - 1))
                if k % CH == CH - 1:
                    last_.then_inc(y_done, 1)

        def max_rows(pe, m, c, unit, bank):
            aux_free(pe, unit)
            pe.wait_ge(msp_ready, 2 * m + c + 1)
            for t in range(4):
                last_ = nc.tensor.transpose(aux[bank][:, P * t:P * t + P], mspread[:, t, :], ident)
            last_.then_inc(aux_ready, 1)

        def values(pe, n, s, parity):
            c, j, q, cols = SUB[s]
            if j == 0:
                wait(pe, ot_evac, 2 * n + c)
            if s == 0:
                pe.wait_ge(v_done, n + 1)
            if s in DIAG:
                pe.wait_ge(sel_done, len(DIAG) * n + DIAG.index(s) + 1)
            else:
                pe.wait_ge(act_done, SC_UNITS * n + NH + HG * (s + 1))
            for h in range(HG):
                last_ = nc.tensor.matmul(ov[32 * h:32 * h + 32, W - cols:W], v[parity][:, j, h, :],
                                         probs[:, s % 2, h, 0:cols], start=(j == 0),
                                         stop=(j == (3 if c == 0 else TPB - 1)))
            last_.then_inc(pv_done, 1)

        def out_rows(pe, n, c, unit, bank):
            aux_free(pe, unit)
            pe.wait_ge(ot_evac, 2 * n + c + 1)
            for t in range(4):
                last_ = nc.tensor.transpose(aux[bank][:, P * t:P * t + P], ot[:, c, P * t:P * t + P], ident)
            last_.then_inc(aux_ready, 1)

        def attn_columns(pe, c, unit, bank, attn_unit):
            aux_free(pe, unit)
            pe.wait_ge(aux_done, attn_unit + 1)
            for t in range(4):
                last_ = nc.tensor.transpose(aux[bank][:, P * t:P * t + P],
                                            attn[:, 4 * c + t].rearrange("p g h d -> p (g h d)"), ident)
            last_.then_inc(aux_ready, 1)

        def project(pe, b, c, unit, bank, column_unit):
            aux_free(pe, unit)
            pe.wait_ge(aux_done, column_unit + 1)
            wait(pe, yadd_done, 2 * (E - 1) * b)
            for t in range(4):
                tok = slice(W * c + P * t, W * c + P * t + P)
                dst = aux[bank][:, P * t:P * t + P]
                nc.tensor.matmul(dst, attnT[:, tok], wp[:, :], start=True, stop=False)
                last_ = nc.tensor.matmul(dst, yT[:, tok], ident, start=False, stop=True)
            last_.then_inc(aux_ready, 1)

        def tensor_batch(b, first, last):
            pe, order, base, par = nc.tensor, aux_order(first, last), aux_base(b), aux_parity(b)
            for g in range(G4):
                n = G4 * b + g
                start = SC_UNITS * n
                token = b * T + W * (g // 2)
                for k in range(NH):
                    if not (first and g == 0 and k < EARLY):
                        hidden(pe, g, token, k, start)
                    if k == 0 and not (first and g == 0):
                        values(pe, n - 1, NS - 1, (g + 1) % 2)
                    what, u = after(g, first).get(k, (None, 0))
                    if what is None or not present(what, g, first, last):
                        continue
                    o = order[what, g, u]
                    unit, bank = base + o, (par + o) % 2
                    if what == "madd1":
                        max_rows(pe, n, 1, unit, bank)
                    elif what == "ot1":
                        out_rows(pe, n - 1, 1, unit, bank)
                    elif what == "prep":
                        prep_product(pe, (g + 1) % G4, u, unit, bank, T * (b + (g + 1) // G4))
                    elif what == "ft":
                        attn_columns(pe, u, unit, bank, base + order["ot1", g, 0])
                    elif what == "fo":
                        project(pe, b, u, unit, bank, base + order["ft", g, u])
                more = present("next", g, first, last)

                pe.wait_ge(aux_done, base + (order["prep", g, 3] if ("prep", g, 3) in order else order["madd1", g, 0]) + 1)
                for s in range(NS):
                    heads, maxima = iter(range(HG)), iter(range(HG))
                    for part in ORDER:
                        if part == "S":
                            scores(pe, g, s, start, next(heads))
                        elif part == "M" and more:
                            h = next(maxima)
                            o = order["max", g, s, h]
                            max_scores(pe, s, h, (g + 1) % 2, base + o, (par + o) % 2)
                        elif part == "Y":
                            output_layer(pe, g, s, n, start, first)
                        elif part == "V" and s:
                            values(pe, n, s - 1, g % 2)
                        elif part == "X" and s in EXTRA and (EXTRA[s], g) in order:
                            o = order[EXTRA[s], g]
                            if EXTRA[s] == "madd0":
                                max_rows(pe, n + 1, 0, base + o, (par + o) % 2)
                            else:
                                out_rows(pe, n, 0, base + o, (par + o) % 2)

        def prep_split(dve, m, u, parity, unit, bank):
            dve.wait_ge(aux_ready, unit + 1)
            dve.wait_ge(hic_done, 4 * m + u + 1)
            wait(dve, sc_ready, SC_UNITS * (m - 1))
            dst = (kT, qT)[u % 2][parity]
            nc.vector.scalar_tensor_tensor(out=dst[:, W * (u // 2):W * (u // 2) + W], in0=aux[bank][:, :],
                                           scalar=lo_row[u % 2], in1=hic[:, u % 2, :],
                                           op0=ALU.mult, op1=ALU.add).then_inc(aux_done, 1)

        def maximum(dve, s, h, unit, bank):
            i, _, cols, diagonal, slot = MAXES[s]
            dve.wait_ge(aux_ready, unit + 1)
            if not diagonal:
                nc.vector.reduce_max(maxes[:, i, slot, h:h + 1], aux[bank][:, 0:cols], axis=AX.X).then_inc(aux_done, 1)
                return
            wait(dve, aux_done, unit - 1)
            if cols > P:
                other = 1 if i < 4 else 2
                nc.vector.reduce_max(maxes[:, i, other, h:h + 1], aux[bank][:, 0:cols - P], axis=AX.X)
            elif not isinstance(unit, int):
                dve.sem_inc(dve_turn, 1)
            nc.vector.tensor_tensor_reduce(out=junk[:, bank, :], in0=aux[bank][:, cols - P:cols], in1=cmask,
                                           scale=1.0, scalar=LOW, op0=ALU.add, op1=ALU.max,
                                           accum_out=maxes[:, i, 0, h:h + 1]).then_inc(aux_done, 1)

        def spread_maxima(dve, m, c, unit):
            dst = mspread[:, :, :].rearrange("p t (h r) -> p t h r", r=32)
            dve.wait_ge(aux_done, unit + 1)
            nc.vector.reduce_max(mrow[:, :, :], maxes[:, 4 * c:4 * c + 4].rearrange("p t s h -> p t h s"),
                                 axis=AX.X).then_inc(mrow_done, 1)
            dve.wait_ge(mrow_done, 2 * m + c + 1)
            nc.vector.tensor_scalar(dst[:, :, :, 24].bitcast(F32R), mrow[:, :, :], -1.0, None, ALU.mult) \
                .then_inc(negh_done, 1)
            dve.wait_ge(negh_done, 2 * m + c + 1)
            nc.vector.scalar_tensor_tensor(out=dst[:, :, :, 25].bitcast(F32R), in0=mrow[:, :, :], scalar=-1.0,
                                           in1=dst[:, :, :, 24], op0=ALU.mult, op1=ALU.subtract).then_inc(msp_ready, 1)

        def add_max_rows(dve, c, parity, unit, bank):
            dst = qT[parity][:, W * c:W * c + W]
            dve.wait_ge(aux_ready, unit + 1)
            nc.vector.tensor_tensor(dst, aux[bank][:, :], dst.bitcast(F32), ALU.add).then_inc(aux_done, 1)

        def normalise(dve, n, g, c, unit, bank):
            src = aux[bank][:, :].rearrange("p (t h r) -> p t h r", h=HG, r=32)
            dve.wait_ge(aux_ready, unit + 1)
            nc.vector.reciprocal(rden[:, :, :], src[:, :, :, D]).then_inc(rden_done, 1)
            dve.wait_ge(rden_done, 2 * n + c + 1)
            nc.vector.tensor_tensor(attn[:, 4 * c:4 * c + 4, g], src[:, :, :, 0:D], bcast(rden[:, :, :], D),
                                    ALU.mult).then_inc(aux_done, 1)

        def finish(dve, b, what, c, unit, bank):
            dve.wait_ge(aux_ready, unit + 1)
            if what == "ft":
                nc.vector.tensor_copy(attnT[:, W * c:W * c + W], aux[bank][:, :]).then_inc(aux_done, 1)
            else:
                dve.wait_ge(xb_done, 2 * b)
                dst = xres[:, c]
                nc.vector.tensor_tensor(dst, aux[bank][:, :].rearrange("p (t c) -> p t c", c=C), dst,
                                        ALU.add).then_inc(aux_done, 1)

        side = [ov, yp]

        def low_part(dve, r):
            dve.wait_ge(xT_ready, r + 1)
            dve.wait_ge(xh_done, r + 1)
            cols = slice(W * r, W * r + W)
            nc.vector.tensor_tensor(xl[:, cols], side[SIDE_BANK["xt", r]][:, :], xh[:, cols].bitcast(F32),
                                    ALU.subtract).then_inc(xl_done, 1)

        def vector_batch(b, first, last):
            dve, order, base, par = nc.vector, aux_order(first, last), aux_base(b), aux_parity(b)
            for g in range(G4):
                n = G4 * b + g
                for k in sorted(after(g, first)):
                    what, u = after(g, first)[k]
                    if not present(what, g, first, last):
                        continue
                    o = order[what, g, u]
                    unit, bank = base + o, (par + o) % 2
                    if what == "madd1":
                        add_max_rows(dve, 1, g % 2, unit, bank)
                    elif what == "ot1":
                        normalise(dve, n - 1, (g - 1) % G4, 1, unit, bank)
                    elif what == "prep":
                        prep_split(dve, n + 1, u, (g + 1) % 2, unit, bank)
                    else:
                        finish(dve, b, what, u, unit, bank)
                more = present("next", g, first, last)
                for s in range(NS):
                    maxima = iter(range(HG))
                    for part in ORDER:
                        if part == "G" and s in YEND:
                            gate_expert(dve, b, g, n, YEND[s])
                        elif part == "M" and more:
                            h = next(maxima)
                            o = order["max", g, s, h]
                            maximum(dve, s, h, base + o, (par + o) % 2)
                        elif part == "X" and s in EXTRA and (EXTRA[s], g) in order:
                            o = order[EXTRA[s], g]
                            if EXTRA[s] == "madd0":
                                add_max_rows(dve, 0, (g + 1) % 2, base + o, (par + o) % 2)
                            else:
                                normalise(dve, n, g, 0, base + o, (par + o) % 2)
                    if more and s in (3, NS - 1):
                        spread_maxima(dve, n + 1, s // 4 // 2, base + order["max", g, s, HG - 1])

        def gate_expert(dve, b, g, n, i):
            e = EG * (g % 2) + i
            adds = (E - 1) * (2 * b + g // 2)
            dve.wait_ge(y_done, EG * n + i + 1)
            dve.wait_ge(gates_loaded, 16 * (n + 1))
            if e > 0:
                wait(dve, yadd_done, adds + (e - 2 if e > 2 else 0))
            dst = yT[:, W * (g // 2):W * (g // 2) + W] if e == 0 else ytmp[:, e % 2, :]
            nc.vector.scalar_tensor_tensor(out=dst.rearrange("p (t q) -> p t q", q=P),
                                           in0=yp[:, :].rearrange("p (t q) -> p t q", q=P),
                                           scalar=b2T[:, e:e + 1], in1=gates[:, :, i, :],
                                           op0=ALU.add, op1=ALU.mult).then_inc(ymul_done, 1)

        @block.sync
        def _(sp):
            for i in range(4):
                sp.dma_start(x_in[:, 8 * i:8 * i + 8, :].rearrange("p (n i) c -> p n i c", i=4),
                             x_v[2 * i:2 * i + 2].rearrange("n p i c -> p n i c")).then_inc(x_loaded[i], 16)
                if i == 0:
                    sp.dma_start(wqkv[:, :], w_qkv).then_inc(w_loaded, 16)
            sp.dma_start(w1_in, W1.rearrange("e h i -> h e i")).then_inc(w1_loaded, 16)
            sp.dma_start(w2[:, :, :], W2.rearrange("e (c p) h -> p (e c) h", p=P)).then_inc(w2_loaded, 16)
            sp.dma_start(wp[:, :], w_proj).then_inc(p_loaded, 16)
            sp.dma_start(bp[:, :], b_proj.partition_broadcast(P)).then_inc(p_loaded, 16)
            for n in range(B):
                sp.wait_ge(vg_done, 4 * (n + 1))
                sp.dma_start(v_scr[G4 * n:G4 * n + G4].rearrange("g p f -> p g f"),
                             v_all[:, n].rearrange("p g t c -> p g (t c)")).then_inc(v_stored, 16)
            sp.wait_ge(v_stored, 16 * B)
            load_v(sp, 0)
            sp.wait_ge(gT_done, 1)
            for k in range(2):
                sp.dma_start(g_scr[16 * k:16 * k + 16].rearrange("t (e p) -> (t e) p", p=P),
                             grow[:, k, :]).then_inc(g_stored, 16)
            sp.wait_ge(g_stored, 32)
            load_gates(sp, 0, 0)
            over_batches(sp, sync_batch)
            tail = aux_base(B - 1) + len(aux_order(False, True))
            load_xres(sp, B)
            for c in range(2):
                sp.wait_ge(aux_done, tail + 4 + c)
                store(sp, B, c)
            sp.wait_ge(stored, 32 * B)

        @block.gpsimd
        def _(pool):
            nc.gpsimd.memset(small[:, :], 0.0).then_inc(small_zero, 1)
            nc.gpsimd.memset(half[:, :], -0.5).then_inc(pchain, 1)
            nc.gpsimd.memset(wkq[:, :, :, :], 0.0).then_inc(wkq_zero, 1)
            nc.gpsimd.memset(mspread[:, :, :], 0.0).then_inc(zeroed, 1)

            def inverse_deviation(i):
                t = slice(8 * i, 8 * i + 8)
                pool.wait_ge(mv_ready, i + 1)
                nc.gpsimd.tensor_scalar(veps[:, t], meanvar[:, t, 1], EPS, None, ALU.add).then_inc(pchain, 1)
                pool.wait_ge(pchain, 2 + i)
                nc.gpsimd.tensor_tensor(rstd[:, t], veps[:, t], half[:, t], ALU.pow).then_inc(rstd_ready, 1)

            inverse_deviation(0)
            pool.wait_ge(wkqh_done, 1)
            nc.gpsimd.tensor_tensor(wkql[:, :, :, :], wkq[:, :, :, :], wkqh[:, :, :, :].bitcast(F32),
                                    ALU.subtract).then_inc(wkq_ready, 1)
            inverse_deviation(1)
            for i in range(2):
                nc.gpsimd.memset(v[i][:, :, :, :], 0.0).then_inc(zeroed, 1)
            inverse_deviation(2)
            for i in range(2):
                if i:
                    inverse_deviation(3)
                pool.wait_ge(w1h_done, i + 1)
                nc.gpsimd.tensor_tensor(w1l[:, 4 * i:4 * i + 4, :], w1_in[:, 4 * i:4 * i + 4, :],
                                        w1h[:, 4 * i:4 * i + 4, :].bitcast(F32), ALU.subtract).then_inc(w1l_done, 1)
            pool.wait_ge(zeroed, 3)
            for i in range(2):
                nc.gpsimd.memset(v[i][:, :, :, D:D + 1], 1.0).then_inc(zeroed, 1)
            expand_v(pool, 0, 0)
            over_batches(pool, pool_batch)
            finish_bias(pool, B)

        @block.scalar
        def _(act):
            act.dma_start(cst[:, :], consts).then_inc(c_loaded, 16)
            act.wait_ge(small_zero, 1)
            act.dma_start(small[0:32, :], b1.rearrange("e (c p) -> (e c) p", p=P)).then_inc(s_loaded, 16)
            act.dma_start(small[32:40, :], b2).then_inc(s_loaded, 16)
            act.dma_start(small[64:72, :], Wg).then_inc(s_loaded, 16)

            def x_hi(r):
                act.wait_ge(xT_ready, r + 1)
                nc.scalar.copy(xh[:, W * r:W * (r + 1)], side[SIDE_BANK["xt", r]][:, :]).then_inc(xh_done, 1)

            act.wait_ge(wkq_laid, 1)
            nc.scalar.copy(wkqh[:, :, :, :], wkq[:, :, :, :]).then_inc(wkqh_done, 1)
            x_hi(0)
            x_hi(1)
            for what, i in SETUP:
                unit = SETUP_AUX.get((what, i))
                if what == "xt":
                    x_hi(i)
                elif what == "prep":
                    prep_hic(act, i, unit, unit % 2, SETUP_AUX["prep", max(i - 2, 0)])
                elif what == "next":
                    act.wait_ge(next_ready, i + 1)
                    if i < 2:
                        act.wait_ge(aux_done, SETUP_AUX["prep", 2 + i] + 1)
                    else:
                        act.wait_ge(next_done, i - 1)
                    nc.scalar.activation(hic[:, i % 2, :].bitcast(F32R), side[i % 2][:, :], ACT.Identity,
                                         bias=ones_row[i % 2], scale=hi_sign[i % 2]).then_inc(hic_done, 1)
                elif what == "max" and i in (2, 4):
                    if i == 2:
                        act.wait_ge(w1_loaded, 16)
                    half_ = slice(0, 4) if i == 2 else slice(4, 8)
                    nc.scalar.copy(w1h[:, half_, :], w1_in[:, half_, :]).then_inc(w1h_done, 1)
                elif what == "vg":
                    act.wait_ge(vg_ready, i + 1)
                    src = side[SIDE_BANK["vg", i]][:, 0:2 * (C + E)].rearrange("p (t n) -> p t n", t=2)
                    n, t = divmod(2 * i, TPB)
                    nc.scalar.copy(v_all[:, n, :, t:t + 2, :].rearrange("p g t c -> p t g c"),
                                   src[:, :, 0:C].rearrange("p t (g c) -> p t g c", c=32))
                    nc.scalar.copy(logits[:, 2 * i:2 * i + 2, :], src[:, :, C:C + E]).then_inc(vg_done, 1)
                elif what == "hid":
                    if i == 0:
                        act.wait_ge(w1l_done, 1)
                        act.wait_ge(smallT_done, 1)
                    if i == 4:
                        act.wait_ge(w1l_done, 2)
                    gelu(act, 0, i, 0)
                elif what == "weigh":
                    act.wait_ge(dlt_ready, 1)
                    nc.scalar.activation(ex, dlt, ACT.Exp).then_inc(ex_ready, 1)
            act.wait_ge(v_stored, 16 * B)
            over_batches(act, act_batch)
            evacuate_ov(act, G4 * B - 1, 1)

        @block.tensor
        def _(pe):
            def side_free(what, r):
                if (what, r) in SIDE_BEFORE:
                    what_, r_ = SIDE_BEFORE[what, r]
                    if what_ == "xt":
                        pe.wait_ge(xl_done, r_ + 1)
                    else:
                        pe.wait_ge(vg_done, r_ + 1)

            def transpose_x(r):
                pe.wait_ge(xn_ready, r + 1)
                side_free("xt", r)
                for t in range(4):
                    last_ = nc.tensor.transpose(side[SIDE_BANK["xt", r]][:, P * t:P * t + P], x_in[:, 4 * r + t, :], ident)
                last_.then_inc(xT_ready, 1)

            def values_logits(r):
                pe.wait_ge(xl_done, r // 2 + 1)
                side_free("vg", r)
                for t in range(2):
                    tok = slice(P * (2 * r + t), P * (2 * r + t) + P)
                    dst = side[SIDE_BANK["vg", r]][:, (C + E) * t:(C + E) * (t + 1)]
                    nc.tensor.matmul(dst, xh[:, tok], wvgh[:, :], start=True, stop=False)
                    nc.tensor.matmul(dst, xh[:, tok], wvgl[:, :], start=False, stop=False)
                    last_ = nc.tensor.matmul(dst, xl[:, tok], wvgh[:, :], start=False, stop=True)
                last_.then_inc(vg_ready, 1)

            pe.wait_ge(c_loaded, 16)
            transpose_x(0)
            transpose_x(1)
            pe.wait_ge(s_loaded, 48)
            nc.tensor.transpose(sc[3][:, 0:P], small[:, :], ident).then_inc(smallT_ready, 1)
            pe.wait_ge(wkq_ready, 1)
            for what, i in SETUP:
                unit = SETUP_AUX.get((what, i))
                if what == "xt":
                    transpose_x(i)
                elif what == "vg":
                    if i == 0:
                        pe.wait_ge(wvg_ready, 1)
                    values_logits(i)
                elif what == "prep":
                    pe.wait_ge(xl_done, i // 2 + 1)
                    prep_product(pe, 0, i, unit, unit % 2, 0)
                elif what == "next":
                    if i == 0:
                        pe.wait_ge(vg_done, NT // 2)
                    if i == 1:
                        pe.wait_ge(gT_done, 1)
                    wait(pe, next_done, i - 1)
                    tok = slice(W * (i // 2), W * (i // 2) + W)
                    split_product(side[i % 2][:, :], wkqh[:, i % 2, 1, :], wkql[:, i % 2, 1, :],
                                  xh[:, tok], xl[:, tok]).then_inc(next_ready, 1)
                elif what == "max":
                    if i in (0, 16):
                        pe.wait_ge(aux_done, SETUP_AUX["prep", 1 if i == 0 else 3] + 1)
                    max_scores(pe, i // HG, i % HG, 0, unit, unit % 2)
                elif what == "madd":
                    max_rows(pe, 0, 0, unit, unit % 2)
                elif what == "hid":
                    if i == 0:
                        pe.wait_ge(w1l_done, 1)
                    hidden(pe, 0, 0, i, 0)
                elif what == "turn_gates":
                    pe.wait_ge(g_ready, 1)
                    for k in range(2):
                        last_ = nc.tensor.transpose(yp[:, P * k:P * k + P],
                                                    g_all[:, 16 * k:16 * k + 16, :].rearrange("p t e -> p (t e)"), ident)
                    last_.then_inc(gT_ready, 1)
            pe.wait_ge(w1l_done, 2)
            pe.wait_ge(next_done, 4)
            pe.wait_ge(w2_loaded, 16)
            pe.wait_ge(p_loaded, 32)
            over_batches(pe, tensor_batch)
            n, unit = G4 * B - 1, aux_base(B - 1) + len(aux_order(False, True))
            values(pe, n, NS - 1, n % 2)
            out_rows(pe, n, 1, unit, unit % 2)
            for c in range(2):
                attn_columns(pe, c, unit + 1 + c, (unit + 1 + c) % 2, unit)
            for c in range(2):
                project(pe, B, c, unit + 3 + c, (unit + 3 + c) % 2, unit + 1 + c)

        @block.vector
        def _(dve):
            links = [0]

            def link(ins):
                links[0] += 1
                ins.then_inc(chain, 1)
                dve.wait_ge(chain, links[0])

            def statistics(i):
                dve.wait_ge(x_loaded[i], 16)
                for t in range(8 * i, 8 * i + 8):
                    last_ = nc.vector.bn_stats(stats[:, t, :], x_in[:, t, :])
                link(last_)
                for t in range(8 * i, 8 * i + 8):
                    last_ = nc.vector.bn_aggr(meanvar[:, t, :], stats[:, t, :])
                last_.then_inc(mv_ready, 1)

            def normalise_x(i):
                dve.wait_ge(mv_ready, i + 1)
                dve.wait_ge(rstd_ready, i + 1)
                for t in range(8 * i, 8 * i + 8):
                    last_ = nc.vector.tensor_scalar(x_in[:, t, :], x_in[:, t, :], meanvar[:, t, 0:1], rstd[:, t:t + 1],
                                                    ALU.subtract, ALU.mult)
                    if t % 4 == 3:
                        last_.then_inc(xn_ready, 1)

            def one_hot(dst, values_, top, rank):
                link(nc.vector.reduce_max(top, values_, axis=AX.X))
                link(nc.vector.tensor_tensor(eq, values_, bcast(top, E), ALU.is_equal))
                link(nc.vector.tensor_tensor(eq, eq, rank8.unsqueeze(1).to_broadcast([P, NT, E]), ALU.mult))
                link(nc.vector.reduce_max(rank, eq, axis=AX.X))
                link(nc.vector.tensor_tensor(dst, eq, bcast(rank, E), ALU.is_equal))

            def top_two():
                dve.wait_ge(vg_done, NT // 2)
                one_hot(first1, logits, top1, c1)
                link(nc.vector.scalar_tensor_tensor(out=rest, in0=first1, scalar=LOW, in1=logits,
                                                    op0=ALU.mult, op1=ALU.add))
                one_hot(first2, rest, top2, c2)
                nc.vector.tensor_tensor(dlt, top2, top1, ALU.subtract).then_inc(dlt_ready, 1)

            def weigh():
                dve.wait_ge(ex_ready, 1)
                link(nc.vector.tensor_scalar(den, ex, 1.0, None, ALU.add))
                link(nc.vector.reciprocal(r1, den))
                link(nc.vector.tensor_tensor(r2, ex, r1, ALU.mult))
                link(nc.vector.tensor_tensor(first1, first1, bcast(r1, E), ALU.mult))
                link(nc.vector.tensor_tensor(first2, first2, bcast(r2, E), ALU.mult))
                nc.vector.tensor_tensor(g_all, first1, first2, ALU.add).then_inc(g_ready, 1)

            nc.vector.memset(maxes[:, :, :, :], LOW)
            statistics(0)
            dve.wait_ge(wkq_zero, 1)
            dve.wait_ge(w_loaded, 16)
            heads = wkq[:, :, :, :].rearrange("p a g (h r) -> p a (g h) r", r=32)
            for kq, (col, scale) in enumerate(((C, 1.0), (0, SCALE))):
                src = wqkv[:, col:col + C].rearrange("p (h d) -> p h d", d=D).unsqueeze(2).to_broadcast([P, H, 3, D])
                last_ = nc.vector.tensor_scalar(heads[:, kq, :, 0:3 * D].rearrange("p h (a d) -> p h a d", d=D), src,
                                                scale, None, ALU.mult)
            last_.then_inc(wkq_laid, 1)
            normalise_x(0)
            statistics(1)
            low_part(dve, 0)
            normalise_x(1)
            low_part(dve, 1)
            dve.wait_ge(smallT_ready, 1)
            link(nc.vector.tensor_copy(smallT[:, :], sc[3][:, 0:72]))
            nc.vector.tensor_copy(wvg[:, 0:C], wqkv[:, 2 * C:3 * C])
            nc.vector.tensor_copy(wvg[:, C:C + E], wgT).then_inc(smallT_done, 1)
            dve.wait_ge(smallT_done, 1)
            link(nc.vector.tensor_copy(wvgh[:, :], wvg[:, :]))
            nc.vector.tensor_tensor(wvgl[:, :], wvg[:, :], wvgh[:, :].bitcast(F32), ALU.subtract).then_inc(wvg_ready, 1)
            dve.wait_ge(c_loaded, 16)
            for what, i in SETUP:
                unit = SETUP_AUX.get((what, i))
                if what == "low":
                    low_part(dve, i)
                elif what == "prep":
                    prep_split(dve, 0, i, 0, unit, unit % 2)
                elif what == "next_split":
                    dve.wait_ge(next_ready, i + 1)
                    dve.wait_ge(hic_done, 4 + i + 1)
                    dst = (kT, qT)[i % 2][1][:, W * (i // 2):W * (i // 2) + W]
                    nc.vector.scalar_tensor_tensor(out=dst, in0=side[i % 2][:, :], scalar=lo_row[i % 2],
                                                   in1=hic[:, i % 2, :], op0=ALU.mult, op1=ALU.add) \
                        .then_inc(next_done, 1)
                elif what == "stats":
                    statistics(i)
                elif what == "norm":
                    normalise_x(i)
                elif what == "max":
                    maximum(dve, i // HG, i % HG, unit, unit % 2)
                    if i == 15:
                        spread_maxima(dve, 0, 0, unit)
                elif what == "madd":
                    add_max_rows(dve, 0, 0, unit, unit % 2)
                elif what == "top_two":
                    top_two()
                elif what == "weigh":
                    weigh()
                elif what == "turn_gates":
                    dve.wait_ge(gT_ready, 1)
                    nc.vector.tensor_copy(grow, yp[:, 0:2 * P].rearrange("p (k q) -> p k q", k=2)).then_inc(gT_done, 1)
            spread_maxima(dve, 0, 1, AUX_START - 1)
            over_batches(dve, vector_batch)
            n, unit = G4 * B - 1, aux_base(B - 1) + len(aux_order(False, True))
            normalise(dve, n, G4 - 1, 1, unit, unit % 2)
            for i, (what, c) in enumerate((("ft", 0), ("ft", 1), ("fo", 0), ("fo", 1))):
                finish(dve, B, what, c, unit + 1 + i, (unit + 1 + i) % 2)


_INS = ["L0_attn_x", "L0_attn_w_qkv", "L0_attn_w_proj", "L0_attn_b_proj", "L0_ffn_Wg", "L0_ffn_W1", "L0_ffn_b1",
        "L0_ffn_W2", "L0_ffn_b2"]


def shape_constants():
    c = np.zeros((P, CONSTS), np.float32)
    c[:, 0:P] = np.eye(P)
    c[:, P:2 * P] = np.triu(np.full((P, P), MASKED), 1)
    row = np.arange(P) % 32
    for kq, lo in enumerate((D, 2 * D)):
        low = (row >= lo) & (row < lo + D)
        c[:, 2 * P + 2 * kq] = low
        c[:, 2 * P + 2 * kq + 1] = 1 - 2 * low
    c[:, 2 * P + 4] = (row == 3 * D) | (row == 3 * D + 1)
    c[:, 2 * P + 6:] = np.arange(E, 0, -1)
    return c


def kernel(**inputs):
    import concourse.bacc as bacc
    from concourse.bass_utils import run_bass_kernel_spmd

    nc = bacc.Bacc("TRN2", target_bir_lowering=False, num_devices=1)
    arrays, args = {}, []
    for name in _INS:
        a = np.ascontiguousarray(inputs[name])
        arrays[f"in_{name}"] = a
        args.append(nc.dram_tensor(f"in_{name}", a.shape, mybir.dt.from_np(a.dtype), kind="ExternalInput").ap())
    arrays["shape_consts"] = shape_constants()
    args.append(nc.dram_tensor("shape_consts", (P, CONSTS), F32, kind="ExternalInput").ap())
    args.append(nc.dram_tensor("out_0", (B, T, C), F32, kind="ExternalOutput").ap())
    layer_kernel(nc, *args)
    r = run_bass_kernel_spmd(nc, [arrays], core_ids=[0])
    return r.results[0]["out_0"]
```
